# Optimizing a Trainium2 kernel written in Bass

```python
import numpy as np
import jax
import jax.numpy as jnp

def _softmax(x, axis=-1):
    return jax.nn.softmax(x, axis=axis)

def _gelu(x):
    return jax.nn.gelu(x, approximate=True)

def _silu(x):
    return jax.nn.silu(x)

def _sigmoid(x):
    return jax.nn.sigmoid(x)

def _layernorm(x, axis=-1, eps=1e-05):
    m = jnp.mean(x, axis=axis, keepdims=True)
    v = jnp.var(x, axis=axis, keepdims=True)
    return (x - m) / jnp.sqrt(v + eps)

def _scatter_add(tgt, idx, src, axis=0):
    return tgt.at[idx].add(src)

def _segment_sum(src, seg, n):
    return jax.ops.segment_sum(src, seg, n)
kernel_name = 'mk_recurrent_d2_jaxref_r8_ffe168'

def setup_inputs(seed: int=0):
    np.random.seed(seed)
    _w = jnp.asarray

    def _L0_attn_setup():
        import jax, jax.numpy as jnp
        import numpy as np
        GAMMA = 0.96875
        H = 128
        B = 4
        L = 256
        key = jax.random.key(seed)
        k0, k1, k2, k3, k4 = jax.random.split(key, 5)
        x = jax.random.normal(k0, (B, L, H), dtype=jnp.float32)
        weight_q = jax.random.normal(k1, (H, H), dtype=jnp.float32) / H
        weight_k = jax.random.normal(k2, (H, H), dtype=jnp.float32) / H
        weight_v = jax.random.normal(k3, (H, H), dtype=jnp.float32) / H
        theta = jax.random.normal(k4, (H,), dtype=jnp.float32) / H
        return {'x': x, 'weight_q': weight_q, 'weight_k': weight_k, 'weight_v': weight_v, 'theta': theta}
    _L0_attn_in = _L0_attn_setup()

    def _L0_ffn_setup():
        import jax, jax.numpy as jnp
        import numpy as np
        D_IN, D_HID = (128, 512)

        def _ternary(key, shape):
            return jax.random.randint(key, shape, -1, 2).astype(jnp.float32)

        def _tlin(x, w, s):
            return jnp.einsum('bsi,oi->bso', x, w) * s
        key = jax.random.key(seed)
        ks = jax.random.split(key, 12)
        inv = lambda fan: 1.0 / np.sqrt(fan).astype(np.float32)
        return {'x': jax.random.normal(ks[0], (4, 256, D_IN), dtype=jnp.float32), 'w1_w': _ternary(ks[1], (D_HID, D_IN)), 'w1_s': jax.random.uniform(ks[2], (D_HID,), dtype=jnp.float32) * inv(D_IN), 'w2_w': _ternary(ks[3], (D_HID, D_IN)), 'w2_s': jax.random.uniform(ks[4], (D_HID,), dtype=jnp.float32) * inv(D_IN), 'h1_w': _ternary(ks[5], (D_HID, D_HID)), 'h1_s': jax.random.uniform(ks[6], (D_HID,), dtype=jnp.float32) * inv(D_HID), 'h2_w': _ternary(ks[7], (D_HID, D_HID)), 'h2_s': jax.random.uniform(ks[8], (D_HID,), dtype=jnp.float32) * inv(D_HID), 'w3_w': _ternary(ks[9], (D_IN, D_HID)), 'w3_s': jax.random.uniform(ks[10], (D_IN,), dtype=jnp.float32) * inv(D_HID)}
    _L0_ffn_in = _L0_ffn_setup()

    def _L1_attn_setup():
        import jax, jax.numpy as jnp
        import numpy as np
        from jax import lax
        B_, L_, D_, N_, K_ = (2, 512, 128, 16, 4)

        def silu(x):
            return x * jax.nn.sigmoid(x)

        def s6_forward(x, W_in, b_in, conv_w, conv_b, W_x, b_x, A_log, D_param, W_out, b_out):
            b, L, D = x.shape
            x_and_gate = x @ W_in + b_in
            x_ssm, gate = jnp.split(x_and_gate, 2, axis=-1)
            xc = jnp.transpose(x_ssm, (0, 2, 1))
            xc = lax.conv_general_dilated(xc, conv_w[:, None, :], window_strides=(1,), padding=[(K_ - 1, 0)], feature_group_count=D, dimension_numbers=('NCH', 'OIH', 'NCH')) + conv_b[None, :, None]
            x_conv = silu(jnp.transpose(xc, (0, 2, 1)))
            BC = x_conv @ W_x + b_x
            B_mat, C_mat = jnp.split(BC, 2, axis=-1)
            A_discrete = jnp.exp(-jnp.exp(A_log))

            def step(h, inp):
                xc_t, B_t, C_t = inp
                h = A_discrete[None] * h + xc_t[:, :, None] * B_t[:, None, :]
                y = jnp.einsum('bn,bdn->bd', C_t, h) + D_param * xc_t
                return (h, y)
            h0 = jnp.zeros((b, D, N_), x.dtype)
            xs = (jnp.transpose(x_conv, (1, 0, 2)), jnp.transpose(B_mat, (1, 0, 2)), jnp.transpose(C_mat, (1, 0, 2)))
            h_final, ys = lax.scan(step, h0, xs)
            y = jnp.transpose(ys, (1, 0, 2))
            y = y * silu(gate)
            y = y @ W_out + b_out
            final_state = h_final.mean(axis=1)
            return (y, final_state)

        def _reference_tuple_inner(x, W_in, b_in, conv_w, conv_b, W_x, b_x, A_log, D_param, W_out, b_out):
            return s6_forward(x, W_in, b_in, conv_w, conv_b, W_x, b_x, A_log, D_param, W_out, b_out)
        key = jax.random.key(seed)
        ks = jax.random.split(key, 11)
        s = lambda fan: 1.0 / np.sqrt(fan)
        return {'x': jax.random.normal(ks[0], (B_, L_, D_), jnp.float32), 'W_in': jax.random.normal(ks[1], (D_, 2 * D_), jnp.float32) * s(D_), 'b_in': jax.random.normal(ks[2], (2 * D_,), jnp.float32) * 0.01, 'conv_w': jax.random.normal(ks[3], (D_, K_), jnp.float32) * s(K_), 'conv_b': jax.random.normal(ks[4], (D_,), jnp.float32) * 0.01, 'W_x': jax.random.normal(ks[5], (D_, 2 * N_), jnp.float32) * s(D_), 'b_x': jax.random.normal(ks[6], (2 * N_,), jnp.float32) * 0.01, 'A_log': jax.random.normal(ks[7], (D_, N_), jnp.float32), 'D_param': jnp.ones((D_,), jnp.float32), 'W_out': jax.random.normal(ks[8], (D_, D_), jnp.float32) * s(D_), 'b_out': jax.random.normal(ks[9], (D_,), jnp.float32) * 0.01}
    _L1_attn_in = _L1_attn_setup()

    def _L1_ffn_setup():
        import jax, jax.numpy as jnp
        import numpy as np
        CAPACITY_FACTOR = 0.5
        key = jax.random.key(seed)
        ks = jax.random.split(key, 5)
        B, S, D, F = (4, 512, 128, 512)
        scale_in = 1.0 / np.sqrt(D)
        scale_ff = 1.0 / np.sqrt(F)
        return {'hidden_states': jax.random.normal(ks[0], (B, S, D), dtype=jnp.float32), 'w_router': jax.random.normal(ks[1], (D,), dtype=jnp.float32) * scale_in, 'W1': jax.random.normal(ks[2], (D, F), dtype=jnp.float32) * scale_in, 'b1': jnp.zeros((F,), dtype=jnp.float32), 'W2': jax.random.normal(ks[3], (F, D), dtype=jnp.float32) * scale_ff, 'b2': jnp.zeros((D,), dtype=jnp.float32)}
    _L1_ffn_in = _L1_ffn_setup()
    _d = {'L0_attn_x': _L0_attn_in['x'], 'L0_attn_weight_q': _L0_attn_in['weight_q'], 'L0_attn_weight_k': _L0_attn_in['weight_k'], 'L0_attn_weight_v': _L0_attn_in['weight_v'], 'L0_attn_theta': _L0_attn_in['theta'], 'L0_ffn_w1_w': _L0_ffn_in['w1_w'], 'L0_ffn_w1_s': _L0_ffn_in['w1_s'], 'L0_ffn_w2_w': _L0_ffn_in['w2_w'], 'L0_ffn_w2_s': _L0_ffn_in['w2_s'], 'L0_ffn_h1_w': _L0_ffn_in['h1_w'], 'L0_ffn_h1_s': _L0_ffn_in['h1_s'], 'L0_ffn_h2_w': _L0_ffn_in['h2_w'], 'L0_ffn_h2_s': _L0_ffn_in['h2_s'], 'L0_ffn_w3_w': _L0_ffn_in['w3_w'], 'L0_ffn_w3_s': _L0_ffn_in['w3_s'], 'L1_attn_W_in': _L1_attn_in['W_in'], 'L1_attn_b_in': _L1_attn_in['b_in'], 'L1_attn_conv_w': _L1_attn_in['conv_w'], 'L1_attn_conv_b': _L1_attn_in['conv_b'], 'L1_attn_W_x': _L1_attn_in['W_x'], 'L1_attn_b_x': _L1_attn_in['b_x'], 'L1_attn_A_log': _L1_attn_in['A_log'], 'L1_attn_D_param': _L1_attn_in['D_param'], 'L1_attn_W_out': _L1_attn_in['W_out'], 'L1_attn_b_out': _L1_attn_in['b_out'], 'L1_ffn_w_router': _L1_ffn_in['w_router'], 'L1_ffn_W1': _L1_ffn_in['W1'], 'L1_ffn_b1': _L1_ffn_in['b1'], 'L1_ffn_W2': _L1_ffn_in['W2'], 'L1_ffn_b2': _L1_ffn_in['b2']}
    _x0 = _d['L0_attn_x']
    _d['L0_attn_x'] = jax.random.normal(jax.random.fold_in(jax.random.key(seed), 1), (4, 1024, 128), dtype=_x0.dtype)
    del _x0
    return _d

def reference(L0_attn_x, L0_attn_weight_q, L0_attn_weight_k, L0_attn_weight_v, L0_attn_theta, L0_ffn_w1_w, L0_ffn_w1_s, L0_ffn_w2_w, L0_ffn_w2_s, L0_ffn_h1_w, L0_ffn_h1_s, L0_ffn_h2_w, L0_ffn_h2_s, L0_ffn_w3_w, L0_ffn_w3_s, L1_attn_W_in, L1_attn_b_in, L1_attn_conv_w, L1_attn_conv_b, L1_attn_W_x, L1_attn_b_x, L1_attn_A_log, L1_attn_D_param, L1_attn_W_out, L1_attn_b_out, L1_ffn_w_router, L1_ffn_W1, L1_ffn_b1, L1_ffn_W2, L1_ffn_b2):

    def _L0_attn_ref(x, weight_q, weight_k, weight_v, theta):
        import jax, jax.numpy as jnp
        import numpy as np
        GAMMA = 0.96875
        H = 128
        B = 4
        L = 256
        Bb, Ll, Hh = x.shape
        dt = x.dtype
        seq = jnp.arange(1, Ll + 1, dtype=dt)
        zero = jnp.asarray(0.0, dtype=dt)
        thetas = jnp.exp(zero * seq[:, None] * theta[None, :])
        theta_conj = thetas
        q = jnp.matmul(x, weight_q) * thetas[None]
        k = jnp.matmul(x, weight_k) * theta_conj[None]
        v = jnp.matmul(x, weight_v)
        n = jnp.arange(Ll)
        diff = n[:, None] - n[None, :]
        D = jnp.where(diff >= 0, jnp.asarray(GAMMA, dt) ** diff.astype(dt), jnp.zeros((), dt))
        scores = jnp.einsum('bid,bjd->bij', q, k) * D[None]
        return jnp.einsum('bij,bjd->bid', scores, v)

    def _L0_ffn_ref(x, w1_w, w1_s, w2_w, w2_s, h1_w, h1_s, h2_w, h2_s, w3_w, w3_s):
        import jax, jax.numpy as jnp
        import numpy as np
        D_IN, D_HID = (128, 512)

        def _ternary(key, shape):
            return jax.random.randint(key, shape, -1, 2).astype(jnp.float32)

        def _tlin(x, w, s):
            return jnp.einsum('bsi,oi->bso', x, w) * s
        h = jax.nn.silu(_tlin(x, w1_w, w1_s)) * _tlin(x, w2_w, w2_s)
        h = jax.nn.gelu(_tlin(h, h1_w, h1_s), approximate=False)
        h = jax.nn.gelu(_tlin(h, h2_w, h2_s), approximate=False)
        return _tlin(h, w3_w, w3_s)

    def _L1_attn_ref(x, W_in, b_in, conv_w, conv_b, W_x, b_x, A_log, D_param, W_out, b_out):
        import jax, jax.numpy as jnp
        import numpy as np
        from jax import lax
        B_, L_, D_, N_, K_ = (2, 512, 128, 16, 4)

        def silu(x):
            return x * jax.nn.sigmoid(x)

        def s6_forward(x, W_in, b_in, conv_w, conv_b, W_x, b_x, A_log, D_param, W_out, b_out):
            b, L, D = x.shape
            x_and_gate = x @ W_in + b_in
            x_ssm, gate = jnp.split(x_and_gate, 2, axis=-1)
            xc = jnp.transpose(x_ssm, (0, 2, 1))
            xc = lax.conv_general_dilated(xc, conv_w[:, None, :], window_strides=(1,), padding=[(K_ - 1, 0)], feature_group_count=D, dimension_numbers=('NCH', 'OIH', 'NCH')) + conv_b[None, :, None]
            x_conv = silu(jnp.transpose(xc, (0, 2, 1)))
            BC = x_conv @ W_x + b_x
            B_mat, C_mat = jnp.split(BC, 2, axis=-1)
            A_discrete = jnp.exp(-jnp.exp(A_log))

            def step(h, inp):
                xc_t, B_t, C_t = inp
                h = A_discrete[None] * h + xc_t[:, :, None] * B_t[:, None, :]
                y = jnp.einsum('bn,bdn->bd', C_t, h) + D_param * xc_t
                return (h, y)
            h0 = jnp.zeros((b, D, N_), x.dtype)
            xs = (jnp.transpose(x_conv, (1, 0, 2)), jnp.transpose(B_mat, (1, 0, 2)), jnp.transpose(C_mat, (1, 0, 2)))
            h_final, ys = lax.scan(step, h0, xs)
            y = jnp.transpose(ys, (1, 0, 2))
            y = y * silu(gate)
            y = y @ W_out + b_out
            final_state = h_final.mean(axis=1)
            return (y, final_state)

        def _reference_tuple_inner(x, W_in, b_in, conv_w, conv_b, W_x, b_x, A_log, D_param, W_out, b_out):
            return s6_forward(x, W_in, b_in, conv_w, conv_b, W_x, b_x, A_log, D_param, W_out, b_out)
        return _reference_tuple_inner(x, W_in, b_in, conv_w, conv_b, W_x, b_x, A_log, D_param, W_out, b_out)[0]

    def _L1_ffn_ref(hidden_states, w_router, W1, b1, W2, b2):
        import jax, jax.numpy as jnp
        import numpy as np
        CAPACITY_FACTOR = 0.5
        'Mixture-of-Depths block: route top-k tokens through an FFN inner block,\n            scatter back with sigmoid router weights; bypassed tokens pass through.'
        B, S, D = hidden_states.shape
        k = int(S * CAPACITY_FACTOR)
        scores = jnp.einsum('bsd,d->bs', hidden_states, w_router)
        top_scores, top_idx = jax.lax.top_k(scores, k)
        weights = jax.nn.sigmoid(top_scores)
        selected = jnp.take_along_axis(hidden_states, top_idx[:, :, None], axis=1)
        h = jax.nn.gelu(jnp.einsum('bkd,df->bkf', selected, W1) + b1)
        processed = jnp.einsum('bkf,fd->bkd', h, W2) + b2
        update = weights[:, :, None] * processed

        def scatter_one(xb, ib, ub):
            return xb.at[ib].add(ub)
        output = jax.vmap(scatter_one)(hidden_states, top_idx, update)
        return output
    x = L0_attn_x
    xn = _layernorm(x, axis=-1)
    s = _L0_attn_ref(xn, L0_attn_weight_q, L0_attn_weight_k, L0_attn_weight_v, L0_attn_theta)
    g = _silu(_L0_ffn_ref(xn, L0_ffn_w1_w, L0_ffn_w1_s, L0_ffn_w2_w, L0_ffn_w2_s, L0_ffn_h1_w, L0_ffn_h1_s, L0_ffn_h2_w, L0_ffn_h2_s, L0_ffn_w3_w, L0_ffn_w3_s))
    x = x + s * g
    xn = _layernorm(x, axis=-1)
    s = _L1_attn_ref(xn, L1_attn_W_in, L1_attn_b_in, L1_attn_conv_w, L1_attn_conv_b, L1_attn_W_x, L1_attn_b_x, L1_attn_A_log, L1_attn_D_param, L1_attn_W_out, L1_attn_b_out)
    g = _silu(_L1_ffn_ref(xn, L1_ffn_w_router, L1_ffn_W1, L1_ffn_b1, L1_ffn_W2, L1_ffn_b2))
    x = x + s * g
    return x

_drawn_inputs = setup_inputs


def setup_inputs(seed=0):
    import zlib

    import numpy as np

    out = dict(_drawn_inputs(seed))
    spreads = {'L1_attn_D_param': (1.0, 0.2), 'L1_ffn_b1': (0.0, 0.1), 'L1_ffn_b2': (0.0, 0.1)}
    factors = {}
    for name, (base, spread) in spreads.items():
        noise = np.random.default_rng([zlib.crc32(name.encode()), seed]).standard_normal(out[name].shape)
        drawn = base * np.exp(spread * noise) if base else spread * noise
        out[name] = jnp.asarray(drawn.astype(out[name].dtype))
    for name, factor in factors.items():
        out[name] = (out[name] * factor).astype(out[name].dtype)
    return out
```

```python
from contextlib import ExitStack

import numpy as np

import concourse.bass as bass
from concourse import mybir

F32 = mybir.dt.float32
BF16 = mybir.dt.bfloat16
ALU = mybir.AluOpType
ACT = mybir.ActivationFunctionType

P = 128
BATCH = 4
SEQ = 1024
HALF = 512
CH = SEQ // P
CPH = HALF // P
HID = 512
KT = HID // P
NSTATE = 16
DPG = P // NSTATE
NGRP = P // DPG
TAPS = 4
CREDIT = 1
MEM_STEPS = CH - 3
TOPK = SEQ // 2
GAMMA = 0.96875
EPS = 1e-5

COLS = {}
_at = 0
for _name, _n in [("w1_s", KT), ("w2_s", KT), ("h1_s", KT), ("h2_s", KT), ("w3_s", 1), ("theta", 1),
                  ("b_in", 2), ("conv_w", TAPS), ("conv_b", 1), ("D", 1), ("b_out", 1), ("b1", KT),
                  ("b2", 1), ("b_x", 2), ("A_log", NGRP), ("gamma_col", 1)]:
    COLS[_name] = slice(_at, _at + _n)
    _at += _n
NCOLS = _at

L0_ACT = ([("xnT", g) for g in range(2)] + [("q", g) for g in range(2)]
          + [("z1", g, m) for g in range(2) for m in range(KT)] + [("u", g) for g in range(2)]
          + [("h1", g, m) for g in range(2) for m in range(KT)]
          + [("h2", g, m) for g in range(2) for m in range(KT)] + [("w3", g) for g in range(2)])
L0_DVE = ([(k, g) for g in range(2) for k in ("scores", "outer")]
          + [("z2", g, m) for g in range(2) for m in range(KT)] + [("s", g) for g in range(2)])
L1_ACT = ([(k, g) for k in ("xnT", "score", "ssm", "B", "C", "gate") for g in range(2)]
          + [("ffn", g, m) for g in range(2) for m in range(KT)])
L1_DVE = ([(k, g) for k in ("tok", "score_col", "rank", "ffn") for g in range(2)]
          + [("xs", gr, g) for gr in range(NGRP) for g in range(2)] + [("out", g) for g in range(2)])


def after(b, order, job):
    return b * len(order) + (order.index(job) + 1 + CREDIT)


def program(nc, x_tok, x_feat, small, w_in0, h_w, w3T, retention_w, l1_w, w2_l1, decay_mask, gamma_row,
            identity, before_mask, spread, gather, out):
    with ExitStack() as ctx:
        def sb(name, shape, dt=F32):
            return ctx.enter_context(nc.sbuf_tensor(name, shape, dt))

        def ps(name, shape, dt=F32):
            return ctx.enter_context(nc.psum_tensor(name, shape, dt))

        def sem(name):
            return ctx.enter_context(nc.semaphore(name))

        col = sb("col", [P, NCOLS])
        w12T = sb("w12T", [P, 2, HID])
        hT = sb("hT", [P, 2, KT, HID])
        w3 = sb("w3", [P, KT, P])
        rw = sb("rw", [P, 3, P])
        lw = sb("lw", [P, 5 * P + P + HID])
        w2l = sb("w2l", [P, KT, P])
        mask = sb("mask", [P, P])
        grow = sb("grow", [P, P])
        ident = sb("ident", [P, P])
        tri = sb("tri", [P, P])
        spr = sb("spr", [P, NGRP, P])
        gat = sb("gat", [P, 2 * P - DPG])
        ones = sb("ones", [P, P], BF16)
        half_neg = sb("half_neg", [P, CH])
        wait_carrier = sb("wait_carrier", [P, 1])
        eps = sb("eps", [P, CH])
        theta1 = sb("theta1", [P, 1])
        wk_th = sb("wk_th", [P, P])
        qk = sb("qk", [P, P])
        aexp = sb("aexp", [P, NGRP])
        decay = sb("decay", [P, NGRP])
        W_IN, W_B, W_C, W_R, W_OUT, W_1 = (lw[:, 0:2 * P], lw[:, 2 * P:3 * P], lw[:, 3 * P:4 * P],
                                           lw[:, 4 * P:5 * P], lw[:, 5 * P:6 * P], lw[:, 6 * P:])

        xt = sb("xt", [P, CH, P])
        xf = sb("xf", [P, SEQ])
        st0 = sb("st0", [P, CH, 6])
        mv0 = sb("mv0", [P, CH, 2])
        ve0 = sb("ve0", [P, CH])
        rstd0 = sb("rstd0", [P, CH])
        xn = sb("xn", [P, CH, P])
        xg = sb("xg", [P, CH, P])
        xnT = sb("xnT", [P, SEQ])
        q = sb("q", [P, SEQ])
        qg = sb("qg", [P, SEQ])
        sc = sb("sc", [P, CH, P])
        mem = sb("mem", [P, CH, P])
        hid0 = sb("hid0", [P, 2, KT, HALF])
        hid1 = sb("hid1", [P, 2, KT, HALF])
        hb = [hid0, hid1, hid0]
        u = qg
        g0 = sb("g0", [P, SEQ])
        x1 = sb("x1", [P, SEQ])
        sg = x1

        st1 = sb("st1", [P, CH, 6])
        mv1 = sb("mv1", [P, CH, 2])
        ve1 = sb("ve1", [P, CH])
        rstd1 = sb("rstd1", [P, CH])
        yn = sb("yn", [P, CH, P])
        tie = yn
        ynT = sb("ynT", [P, SEQ])
        srow = sb("srow", [P, SEQ])
        scol = sb("scol", [P, CH])
        beats = sb("beats", [P, CH, SEQ], BF16)
        ssm = sb("ssm", [P, TAPS - 1 + SEQ])
        xc = sb("xc", [P, SEQ])
        Bt = sb("Bt", [P, SEQ])
        Ct = sb("Ct", [P, SEQ])
        gate = sb("gate", [P, SEQ])
        fh = sb("fh", [P, KT, HALF])
        g1 = sb("g1", [P, SEQ])
        sig = wgt = upd = mod = sigh = g1
        hs = sb("hs", [P, 2, SEQ])
        pr = sb("pr", [P, 2, SEQ])
        yg = sb("yg", [P, SEQ])
        yd = yg
        cv = [yg, xc]
        o = sb("o", [P, SEQ])
        t1 = o

        bank0a = [ps(f"bank0a{i}", [P, HALF]) for i in range(2)]
        bank0d = ps("bank0d", [P, HALF])
        bank1a = ps("bank1a", [P, HALF])
        bank1d = [ps(f"bank1d{i}", [P, HALF]) for i in range(2)]
        ybank = [ps(f"ybank{i}", [P, HALF]) for i in range(2)]

        params = sem("params")
        x_tok_in = sem("x_tok_in")
        x_feat_in = sem("x_feat_in")
        stored = sem("stored")
        consts_set = sem("consts_set")
        theta_ready = sem("theta_ready")
        wk_ready = sem("wk_ready")
        qk_full = sem("qk_full")
        qk_ready = sem("qk_ready")
        aexp_ready = sem("aexp_ready")
        decay_ready = sem("decay_ready")
        l0_act_full = sem("l0_act_full")
        l0_act_done = sem("l0_act_done")
        l0_dve_full = sem("l0_dve_full")
        l0_dve_done = sem("l0_dve_done")
        l1_act_full = sem("l1_act_full")
        l1_act_done = sem("l1_act_done")
        l1_dve_full = sem("l1_dve_full")
        l1_dve_done = sem("l1_dve_done")
        stats0 = sem("stats0")
        aggr0 = sem("aggr0")
        eps0 = sem("eps0")
        rstd0_ready = sem("rstd0_ready")
        xn_ready = sem("xn_ready")
        xg_ready = sem("xg_ready")
        qg_ready = sem("qg_ready")
        mem_step = sem("mem_step")
        x1_ready = sem("x1_ready")
        stats1 = sem("stats1")
        aggr1 = sem("aggr1")
        eps1 = sem("eps1")
        rstd1_ready = sem("rstd1_ready")
        tie_ready = sem("tie_ready")
        beats_ready = sem("beats_ready")
        sig_ready = sem("sig_ready")
        sigh_ready = sem("sigh_ready")
        conv_step = sem("conv_step")
        xc_ready = sem("xc_ready")
        mod_ready = sem("mod_ready")
        g1_ready = sem("g1_ready")
        u_ready = sem("u_ready")
        p_ready = sem("p_ready")
        y_full = sem("y_full")
        yd_ready = sem("yd_ready")
        yg_ready = sem("yg_ready")
        o_ready = sem("o_ready")

        NPARAM = 13
        hs_ = lambda g: slice(g * HALF, (g + 1) * HALF)
        ck = lambda c: slice(c * P, (c + 1) * P)
        block = ctx.enter_context(nc.Block())

        @block.sync
        def _(sp):
            sp.dma_start(col[:], small).then_inc(params, 16)
            sp.dma_start(ident[:], identity).then_inc(params, 16)
            for semaphore in (stored,):
                sp.sem_inc(semaphore, CREDIT)
            with sp.Fori(0, BATCH) as b:
                sp.wait_ge(xn_ready, b * 2 + CREDIT)
                sp.dma_start(xt[:], x_tok[bass.ds(b, 1)].rearrange("o p c d -> (o p) c d")).then_inc(x_tok_in, 16)
                sp.wait_ge(x1_ready, b * 2 + CREDIT)
                sp.dma_start(xf[:], x_feat[bass.ds(b, 1)].rearrange("o p t -> (o p) t")).then_inc(x_feat_in, 16)
                for g in range(2):
                    sp.wait_ge(o_ready, b * 2 + (g + 1) + CREDIT)
                    sp.dma_start(out[bass.ds(b, 1), :, hs_(g)].rearrange("o p t -> (o p) t"), o[:, hs_(g)]).then_inc(stored, 16)
            sp.wait_ge(stored, BATCH * 2 * 16 + CREDIT)

        @block.gpsimd
        def _(pool):
            pool.memset(ones[:], 1.0).then_inc(consts_set, 1)
            pool.memset(half_neg[:], -0.5).then_inc(consts_set, 1)
            pool.memset(eps[:], EPS).then_inc(consts_set, 1)
            pool.memset(mem[:, 0, :], 0.0).then_inc(consts_set, 1)
            pool.memset(ssm[:, 0:TAPS - 1], 0.0).then_inc(consts_set, 1)

            def rstd_l0(b):
                pool.wait_ge(aggr0, b + 1 + CREDIT)
                pool.wait_ge(xn_ready, b * 2 + CREDIT)
                pool.tensor_tensor(ve0[:], mv0[:, :, 1], eps[:], ALU.add).then_inc(eps0, 1)
                pool.wait_ge(eps0, b + 1 + CREDIT)
                pool.tensor_tensor(rstd0[:], ve0[:], half_neg[:], ALU.pow).then_inc(rstd0_ready, 1)

            def scale_q(b):
                for g in range(2):
                    pool.wait_ge(l0_act_done, after(b, L0_ACT, ("q", g)))
                    v = lambda t: t[:, hs_(g)].rearrange("p (c i) -> p c i", i=P)
                    pool.tensor_tensor(v(qg), v(q), grow[:].rearrange("p (o i) -> p o i", o=1).broadcast_to([P, CPH, P]),
                                       ALU.mult).then_inc(qg_ready, 1)

            def rstd_l1(b):
                for g in range(2):
                    c = slice(g * CPH, (g + 1) * CPH)
                    pool.wait_ge(aggr1, b * 2 + (g + 1) + CREDIT)
                    pool.tensor_tensor(ve1[:, c], mv1[:, c, 1], eps[:, c], ALU.add).then_inc(eps1, 1)
                    pool.wait_ge(eps1, b * 2 + (g + 1) + CREDIT)
                    pool.tensor_tensor(rstd1[:, c], ve1[:, c], half_neg[:, c], ALU.pow).then_inc(rstd1_ready, 1)

            def weigh_states(b):
                pool.wait_ge(l1_act_done, after(b, L1_ACT, ("C", 1)))
                for gr in range(NGRP):
                    pool.wait_ge(l1_dve_done, after(b, L1_DVE, ("xs", gr, 1)))
                    if gr >= 2:
                        pool.wait_ge(y_full, b * NGRP + (gr - 1) + CREDIT)
                    else:
                        pool.wait_ge(y_full, b * NGRP + CREDIT)
                    pool.tensor_tensor(pr[:, gr % 2, :], hs[:, gr % 2, :], Ct[:], ALU.mult).then_inc(p_ready, 1)

            pool.wait_ge(consts_set, 5)
            for semaphore in (eps0, rstd0_ready, qg_ready, eps1, rstd1_ready, p_ready):
                pool.sem_inc(semaphore, CREDIT)
            with pool.Fori(0, BATCH) as b:
                rstd_l0(b)
                scale_q(b)
                rstd_l1(b)
                weigh_states(b)

        @block.scalar
        def _(act):
            for dst, src in ((rw, retention_w), (w12T, w_in0), (mask, decay_mask), (grow, gamma_row), (hT, h_w),
                             (w3, w3T), (lw, l1_w), (spr, spread), (gat, gather), (tri, before_mask), (w2l, w2_l1)):
                act.dma_start(dst[:], src).then_inc(params, 16)
            act.wait_ge(params, 16 * NPARAM)
            act.activation(theta1[:], col[:, COLS["theta"]], ACT.Exp, scale=0.0).then_inc(theta_ready, 1)
            act.activation(aexp[:], col[:, COLS["A_log"]], ACT.Exp).then_inc(aexp_ready, 1)
            act.wait_ge(aexp_ready, 1)
            act.activation(decay[:], aexp[:], ACT.Exp, scale=-1.0).then_inc(decay_ready, 1)

            def take0(b, job, out_ap, func=ACT.Copy, **kw):
                act.wait_ge(l0_act_full, after(b, L0_ACT, job))
                act.activation(out_ap, bank0a[L0_ACT.index(job) % 2][:], func, **kw).then_inc(l0_act_done, 1)

            def take1(b, job, out_ap, func=ACT.Copy, **kw):
                act.wait_ge(l1_act_full, after(b, L1_ACT, job))
                act.activation(out_ap, bank1a[:], func, **kw).then_inc(l1_act_done, 1)

            def scale(name, m=0):
                s = COLS[name].start + m
                return col[:, s:s + 1]

            for semaphore in (l0_act_done, l1_act_done, xc_ready, sig_ready, g1_ready):
                act.sem_inc(semaphore, CREDIT)
            with act.Fori(0, BATCH) as b:
                for g in range(2):
                    take0(b, ("xnT", g), xnT[:, hs_(g)])
                for g in range(2):
                    act.wait_ge(qg_ready, b * 2 + CREDIT)
                    take0(b, ("q", g), q[:, hs_(g)])
                for g in range(2):
                    for m in range(KT):
                        act.wait_ge(l0_dve_done, b * len(L0_DVE) + CREDIT)
                        take0(b, ("z1", g, m), hid0[:, g, m, :], ACT.Silu, scale=scale("w1_s", m))
                for g in range(2):
                    take0(b, ("u", g), u[:, hs_(g)])
                for i, k in ((1, "h1"), (2, "h2")):
                    for g in range(2):
                        for m in range(KT):
                            take0(b, (k, g, m), hb[i][:, g, m, :], ACT.Gelu, scale=scale(k + "_s", m))
                for g in range(2):
                    act.wait_ge(x1_ready, b * 2 + CREDIT)
                    take0(b, ("w3", g), g0[:, hs_(g)], ACT.Silu, scale=scale("w3_s"))
                for g in range(2):
                    act.wait_ge(mod_ready, b * 2 + CREDIT)
                    take1(b, ("xnT", g), ynT[:, hs_(g)])
                for g in range(2):
                    act.wait_ge(beats_ready, b + CREDIT)
                    take1(b, ("score", g), srow[:, hs_(g)])
                for g in range(2):
                    act.wait_ge(conv_step, b * TAPS + CREDIT)
                    take1(b, ("ssm", g), ssm[:, TAPS - 1 + g * HALF:TAPS - 1 + (g + 1) * HALF], ACT.Identity,
                          bias=scale("b_in"))
                act.wait_ge(conv_step, b * TAPS + TAPS + CREDIT)
                act.wait_ge(yd_ready, b * 2 + CREDIT)
                act.activation(xc[:], cv[(TAPS - 1) % 2][:], ACT.Silu, bias=scale("conv_b")).then_inc(xc_ready, 1)
                for g in range(2):
                    act.wait_ge(u_ready, b * 2 * NGRP + CREDIT)
                    take1(b, ("B", g), Bt[:, hs_(g)], ACT.Identity, bias=scale("b_x"))
                for g in range(2):
                    act.wait_ge(p_ready, b * NGRP + CREDIT)
                    take1(b, ("C", g), Ct[:, hs_(g)], ACT.Identity, bias=scale("b_x", 1))
                for g in range(2):
                    act.wait_ge(yg_ready, b * 2 + CREDIT)
                    take1(b, ("gate", g), gate[:, hs_(g)], ACT.Silu, bias=scale("b_in", 1))
                act.wait_ge(o_ready, b * 2 + CREDIT)
                act.activation(sig[:], srow[:], ACT.Tanh, scale=0.5).then_inc(sig_ready, 1)
                for g in range(2):
                    if g == 1:
                        act.wait_ge(l1_dve_full, after(b, L1_DVE, ("ffn", 0)))
                    for m in range(KT):
                        take1(b, ("ffn", g, m), fh[:, m, :], ACT.Gelu_apprx_tanh, bias=scale("b1", m))
                for g in range(2):
                    act.wait_ge(mod_ready, b * 2 + (g + 1) + CREDIT)
                    act.wait_ge(o_ready, b * 2 + CREDIT)
                    act.activation(g1[:, hs_(g)], mod[:, hs_(g)], ACT.Silu).then_inc(g1_ready, 1)

        @block.tensor
        def _(pe):
            def open0a(b, job):
                i = L0_ACT.index(job)
                if i >= 2:
                    pe.wait_ge(l0_act_done, b * len(L0_ACT) + (i - 1) + CREDIT)
                else:
                    pe.wait_ge(l0_act_done, b * len(L0_ACT) + CREDIT)
                return bank0a[i % 2]

            def open0d(b, job):
                pe.wait_ge(l0_dve_done, b * len(L0_DVE) + L0_DVE.index(job) + CREDIT)
                return bank0d

            def open1a(b, job):
                pe.wait_ge(l1_act_done, b * len(L1_ACT) + L1_ACT.index(job) + CREDIT)
                return bank1a

            def open1d(b, job):
                i = L1_DVE.index(job)
                if i >= 2:
                    pe.wait_ge(l1_dve_done, b * len(L1_DVE) + (i - 1) + CREDIT)
                else:
                    pe.wait_ge(l1_dve_done, b * len(L1_DVE) + CREDIT)
                return bank1d[i % 2]

            pe.wait_ge(wk_ready, 1)
            pe.matmul(bank0d[:, 0:P], rw[:, 0, :], wk_th[:], start=True, stop=True).then_inc(qk_full, 1)
            pe.wait_ge(qk_ready, 1)
            pe.wait_ge(consts_set, 5)
            for semaphore in (l0_act_full, l0_dve_full, l1_act_full, l1_dve_full, y_full):
                pe.sem_inc(semaphore, CREDIT)
            with pe.Fori(0, BATCH) as b:
                for g in range(2):
                    pe.wait_ge(xn_ready, b * 2 + (g + 1) + CREDIT)
                    bank = open0a(b, ("xnT", g))
                    for c in range(CPH):
                        last = pe.transpose(bank[:, ck(c)], xn[:, g * CPH + c, :], ident[:])
                    last.then_inc(l0_act_full, 1)
                for g in range(2):
                    bank = open0a(b, ("q", g))
                    pe.wait_ge(l0_act_done, after(b, L0_ACT, ("xnT", g)))
                    pe.matmul(bank[:], qk[:], xnT[:, hs_(g)], start=True, stop=True).then_inc(l0_act_full, 1)
                pe.wait_ge(xg_ready, b + 1 + CREDIT)
                for g in range(2):
                    bank = open0d(b, ("scores", g))
                    pe.wait_ge(l0_act_done, after(b, L0_ACT, ("q", g)))
                    for c in range(g * CPH, (g + 1) * CPH):
                        last = pe.matmul(bank[:, ck(c - g * CPH)], xnT[:, ck(c)], q[:, ck(c)], start=True, stop=True)
                    last.then_inc(l0_dve_full, 1)
                    bank = open0d(b, ("outer", g))
                    for c in range(g * CPH, (g + 1) * CPH):
                        last = pe.matmul(bank[:, ck(c - g * CPH)], xg[:, c, :], xn[:, c, :], start=True, stop=True)
                    last.then_inc(l0_dve_full, 1)
                for g in range(2):
                    for m in range(KT):
                        bank = open0a(b, ("z1", g, m))
                        pe.matmul(bank[:], w12T[:, 0, ck(m)], xnT[:, hs_(g)], start=True, stop=True).then_inc(l0_act_full, 1)
                        bank = open0d(b, ("z2", g, m))
                        pe.matmul(bank[:], w12T[:, 1, ck(m)], xnT[:, hs_(g)], start=True, stop=True).then_inc(l0_dve_full, 1)
                for g in range(2):
                    bank = open0a(b, ("u", g))
                    pe.wait_ge(qg_ready, b * 2 + (g + 1) + CREDIT)
                    for c in range(g * CPH, (g + 1) * CPH):
                        pe.matmul(bank[:, ck(c - g * CPH)], xn[:, c, :], sc[:, c, :], start=True, stop=False)
                        last = pe.matmul(bank[:, ck(c - g * CPH)], mem[:, c, :], qg[:, ck(c)], start=False, stop=True)
                    last.then_inc(l0_act_full, 1)
                for i, k in ((0, "h1"), (1, "h2")):
                    for g in range(2):
                        for m in range(KT):
                            bank = open0a(b, (k, g, m))
                            if i == 0:
                                pe.wait_ge(l0_dve_done, after(b, L0_DVE, ("z2", g, KT - 1)))
                            else:
                                pe.wait_ge(l0_act_done, after(b, L0_ACT, ("h1", g, KT - 1)))
                            for kt in range(KT):
                                last = pe.matmul(bank[:], hT[:, i, kt, ck(m)], hb[i][:, g, kt, :],
                                                 start=(kt == 0), stop=(kt == KT - 1))
                            last.then_inc(l0_act_full, 1)
                for g in range(2):
                    bank = open0a(b, ("w3", g))
                    pe.wait_ge(l0_act_done, after(b, L0_ACT, ("h2", g, KT - 1)))
                    for kt in range(KT):
                        last = pe.matmul(bank[:], w3[:, kt, :], hb[2][:, g, kt, :], start=(kt == 0), stop=(kt == KT - 1))
                    last.then_inc(l0_act_full, 1)
                for g in range(2):
                    bank = open0d(b, ("s", g))
                    pe.wait_ge(l0_act_done, after(b, L0_ACT, ("u", g)))
                    pe.matmul(bank[:], rw[:, 2, :], u[:, hs_(g)], start=True, stop=True).then_inc(l0_dve_full, 1)

                for g in range(2):
                    bank = open1d(b, ("tok", g))
                    pe.wait_ge(x1_ready, b * 2 + (g + 1) + CREDIT)
                    for c in range(CPH):
                        last = pe.transpose(bank[:, ck(c)], x1[:, ck(g * CPH + c)], ident[:])
                    last.then_inc(l1_dve_full, 1)
                for g in range(2):
                    bank = open1a(b, ("xnT", g))
                    pe.wait_ge(l1_dve_done, after(b, L1_DVE, ("tok", g)))
                    for c in range(CPH):
                        last = pe.transpose(bank[:, ck(c)], yn[:, g * CPH + c, :], ident[:])
                    last.then_inc(l1_act_full, 1)

                def project(job, g, w):
                    bank = open1a(b, (job, g))
                    pe.wait_ge(l1_act_done, after(b, L1_ACT, ("xnT", g)))
                    pe.matmul(bank[:], w, ynT[:, hs_(g)], start=True, stop=True).then_inc(l1_act_full, 1)

                for g in range(2):
                    project("score", g, W_R)
                for g in range(2):
                    bank = open1d(b, ("score_col", g))
                    pe.wait_ge(l1_act_done, after(b, L1_ACT, ("score", g)))
                    for c in range(CPH):
                        last = pe.transpose(bank[:, ck(c)], srow[:, ck(g * CPH + c)], ident[:])
                    last.then_inc(l1_dve_full, 1)
                for g in range(2):
                    project("ssm", g, W_IN[:, 0:P])
                for job, w in (("B", W_B), ("C", W_C)):
                    for g in range(2):
                        bank = open1a(b, (job, g))
                        pe.wait_ge(xc_ready, b + 1 + CREDIT)
                        pe.matmul(bank[:], w, xc[:, hs_(g)], start=True, stop=True).then_inc(l1_act_full, 1)
                for g in range(2):
                    project("gate", g, W_IN[:, P:2 * P])
                for g in range(2):
                    bank = open1d(b, ("rank", g))
                    pe.wait_ge(beats_ready, b + 1 + CREDIT)
                    for c in range(CH):
                        last = pe.matmul(bank[:], ones[:], beats[:, c, hs_(g)], start=(c == 0), stop=(c == CH - 1))
                    last.then_inc(l1_dve_full, 1)
                for g in range(2):
                    for m in range(KT):
                        bank = open1a(b, ("ffn", g, m))
                        pe.matmul(bank[:], W_1[:, ck(m)], ynT[:, hs_(g)], start=True, stop=True).then_inc(l1_act_full, 1)
                    bank = open1d(b, ("ffn", g))
                    pe.wait_ge(l1_act_done, after(b, L1_ACT, ("ffn", g, KT - 1)))
                    for kt in range(KT):
                        last = pe.matmul(bank[:], w2l[:, kt, :], fh[:, kt, :], start=(kt == 0), stop=(kt == KT - 1))
                    last.then_inc(l1_dve_full, 1)

                def spread_x(gr):
                    for g in range(2):
                        bank = open1d(b, ("xs", gr, g))
                        pe.matmul(bank[:], spr[:, gr, :], xc[:, hs_(g)], start=True, stop=True).then_inc(l1_dve_full, 1)

                def gather_y(gr):
                    if gr == 0:
                        pe.wait_ge(yd_ready, b * 2 + CREDIT)
                    pe.wait_ge(p_ready, b * NGRP + (gr + 1) + CREDIT)
                    for g in range(2):
                        last = pe.matmul(ybank[g][:], gat[:, P - DPG * (gr + 1):2 * P - DPG * (gr + 1)], pr[:, gr % 2, hs_(g)],
                                         start=(gr == 0), stop=(gr == NGRP - 1))
                    last.then_inc(y_full, 1)

                spread_x(0)
                for gr in range(1, NGRP):
                    spread_x(gr)
                    gather_y(gr - 1)
                gather_y(NGRP - 1)
                for g in range(2):
                    bank = open1d(b, ("out", g))
                    pe.wait_ge(yg_ready, b * 2 + (g + 1) + CREDIT)
                    pe.matmul(bank[:], W_OUT, yg[:, hs_(g)], start=True, stop=True).then_inc(l1_dve_full, 1)

        @block.vector
        def _(dve):
            dve.wait_ge(params, 16 * NPARAM)
            dve.wait_ge(theta_ready, 1)
            dve.tensor_scalar(wk_th[:], rw[:, 1, :], theta1[:, 0:1], theta1[:, 0:1], ALU.mult, ALU.mult).then_inc(wk_ready, 1)
            dve.wait_ge(qk_full, 1)
            dve.tensor_copy(qk[:], bank0d[:, 0:P]).then_inc(qk_ready, 1)
            dve.wait_ge(consts_set, 5)
            dve.wait_ge(decay_ready, 1)

            def scale(name, m=0):
                s = COLS[name].start + m
                return col[:, s:s + 1]

            def full0(b, job):
                dve.wait_ge(l0_dve_full, after(b, L0_DVE, job))

            def full1(b, job):
                dve.wait_ge(l1_dve_full, after(b, L1_DVE, job))
                return bank1d[L1_DVE.index(job) % 2]

            for semaphore in (stats0, aggr0, xn_ready, xg_ready, l0_dve_done, mem_step, x1_ready, stats1, aggr1, l1_dve_done, tie_ready, beats_ready, sigh_ready, conv_step, mod_ready, u_ready, yd_ready, yg_ready, o_ready):
                dve.sem_inc(semaphore, CREDIT)
            with dve.Fori(0, BATCH) as b:
                dve.wait_ge(x_tok_in, b * 16 + 16)
                for c in range(CH):
                    last = dve.bn_stats(st0[:, c, :], xt[:, c, :])
                last.then_inc(stats0, 1)
                dve.wait_ge(stats0, b + 1 + CREDIT)
                dve.memset(wait_carrier[:], 0.0)
                for c in range(CH):
                    last = dve.bn_aggr(mv0[:, c, :], st0[:, c, :])
                last.then_inc(aggr0, 1)
                dve.wait_ge(rstd0_ready, b + 1 + CREDIT)
                dve.wait_ge(aggr0, b + 1 + CREDIT)
                for g in range(2):
                    for c in range(g * CPH, (g + 1) * CPH):
                        last = dve.tensor_scalar(xn[:, c, :], xt[:, c, :], mv0[:, c, 0:1], rstd0[:, c:c + 1],
                                                 ALU.subtract, ALU.mult)
                    last.then_inc(xn_ready, 1)
                dve.wait_ge(xn_ready, b * 2 + 2 + CREDIT)
                dve.tensor_scalar(xg[:], xn[:], scale("gamma_col"), None, ALU.mult).then_inc(xg_ready, 1)
                for g in range(2):
                    cs = slice(g * CPH, (g + 1) * CPH)
                    full0(b, ("scores", g))
                    dve.tensor_tensor(sc[:, cs, :], bank0d[:].rearrange("p (c i) -> p c i", i=P),
                                      mask[:].rearrange("p (o i) -> p o i", o=1).broadcast_to([P, CPH, P]),
                                      ALU.mult).then_inc(l0_dve_done, 1)
                    full0(b, ("outer", g))
                    for c in range(g * CPH, (g + 1) * CPH):
                        if c == CPH:
                            dve.wait_ge(l0_dve_done, after(b, L0_DVE, ("outer", 0)))
                        elif c > 0:
                            dve.wait_ge(mem_step, b * MEM_STEPS + (c - g) + CREDIT)
                        last = dve.scalar_tensor_tensor(mem[:, c + 1, :], mem[:, c, :], GAMMA ** P,
                                                        bank0d[:, ck(c - g * CPH)], ALU.mult, ALU.add)
                        if c + 1 in ((g + 1) * CPH, CH - 1):
                            last.then_inc(l0_dve_done, 1)
                            break
                        last.then_inc(mem_step, 1)
                for g in range(2):
                    for m in range(KT):
                        full0(b, ("z2", g, m))
                        dve.wait_ge(l0_act_done, after(b, L0_ACT, ("z1", g, m)))
                        dve.scalar_tensor_tensor(hb[0][:, g, m, :], bank0d[:], scale("w2_s", m), hid0[:, g, m, :],
                                                 ALU.mult, ALU.mult).then_inc(l0_dve_done, 1)
                for g in range(2):
                    full0(b, ("s", g))
                    dve.wait_ge(l0_act_done, after(b, L0_ACT, ("w3", g)))
                    dve.wait_ge(o_ready, b * 2 + CREDIT)
                    dve.tensor_tensor(sg[:, hs_(g)], bank0d[:], g0[:, hs_(g)], ALU.mult).then_inc(l0_dve_done, 1)
                    dve.wait_ge(l0_dve_done, after(b, L0_DVE, ("s", g)))
                    dve.wait_ge(x_feat_in, b * 16 + 16)
                    dve.tensor_tensor(x1[:, hs_(g)], sg[:, hs_(g)], xf[:, hs_(g)], ALU.add).then_inc(x1_ready, 1)

                for g in range(2):
                    bank = full1(b, ("tok", g))
                    for c in range(g * CPH, (g + 1) * CPH):
                        last = dve.bn_stats(st1[:, c, :], bank[:, ck(c - g * CPH)])
                    last.then_inc(stats1, 1)
                    dve.wait_ge(stats1, b * 2 + (g + 1) + CREDIT)
                    dve.memset(wait_carrier[:], 0.0)
                    for c in range(g * CPH, (g + 1) * CPH):
                        last = dve.bn_aggr(mv1[:, c, :], st1[:, c, :])
                    last.then_inc(aggr1, 1)
                for g in range(2):
                    bank = bank1d[L1_DVE.index(("tok", g)) % 2]
                    dve.wait_ge(rstd1_ready, b * 2 + (g + 1) + CREDIT)
                    dve.wait_ge(aggr1, b * 2 + (g + 1) + CREDIT)
                    for c in range(g * CPH, (g + 1) * CPH):
                        last = dve.tensor_scalar(yn[:, c, :], bank[:, ck(c - g * CPH)], mv1[:, c, 0:1],
                                                 rstd1[:, c:c + 1], ALU.subtract, ALU.mult)
                    last.then_inc(l1_dve_done, 1)
                for g in range(2):
                    bank = full1(b, ("score_col", g))
                    dve.tensor_copy(scol[:, g * CPH:(g + 1) * CPH],
                                    bank[:].rearrange("p (c i) -> p c i", i=P)[:, :, 0]).then_inc(l1_dve_done, 1)
                dve.wait_ge(l1_act_done, after(b, L1_ACT, ("ssm", 1)))
                dve.tensor_scalar(cv[0][:], ssm[:, 0:SEQ], scale("conv_w", 0), None, ALU.mult).then_inc(conv_step, 1)
                for k in range(1, TAPS):
                    dve.wait_ge(conv_step, b * TAPS + k + CREDIT)
                    dve.scalar_tensor_tensor(cv[k % 2][:], ssm[:, k:k + SEQ], scale("conv_w", k), cv[(k + 1) % 2][:],
                                             ALU.mult, ALU.add).then_inc(conv_step, 1)
                dve.wait_ge(l1_dve_done, after(b, L1_DVE, ("score_col", 1)))
                for c in range(CH):
                    dve.scalar_tensor_tensor(tie[:, c, :], srow[:, ck(c)], scol[:, c:c + 1], tri[:],
                                             ALU.is_equal, ALU.mult).then_inc(tie_ready, 1)
                for c in range(CH):
                    s_i = scol[:, c:c + 1]
                    if c > 0:
                        dve.tensor_scalar(beats[:, c, 0:c * P], srow[:, 0:c * P], s_i, None, ALU.is_lt)
                    if c < CH - 1:
                        dve.tensor_scalar(beats[:, c, (c + 1) * P:], srow[:, (c + 1) * P:], s_i, None, ALU.is_le)
                    dve.wait_ge(tie_ready, b * CH + (c + 1) + CREDIT)
                    last = dve.scalar_tensor_tensor(beats[:, c, ck(c)], srow[:, ck(c)], s_i, tie[:, c, :],
                                                    ALU.is_lt, ALU.add)
                last.then_inc(beats_ready, 1)
                dve.wait_ge(sig_ready, b + 1 + CREDIT)
                dve.tensor_scalar(sigh[:], sig[:], 0.5, 0.5, ALU.mult, ALU.add).then_inc(sigh_ready, 1)
                dve.wait_ge(sigh_ready, b + 1 + CREDIT)
                for g in range(2):
                    bank = full1(b, ("rank", g))
                    dve.scalar_tensor_tensor(wgt[:, hs_(g)], bank[:], float(TOPK), sigh[:, hs_(g)],
                                             ALU.is_lt, ALU.mult).then_inc(l1_dve_done, 1)
                for g in range(2):
                    bank = full1(b, ("ffn", g))
                    dve.wait_ge(l1_dve_done, after(b, L1_DVE, ("rank", g)))
                    dve.scalar_tensor_tensor(upd[:, hs_(g)], bank[:], scale("b2"), wgt[:, hs_(g)],
                                             ALU.add, ALU.mult).then_inc(l1_dve_done, 1)
                for g in range(2):
                    dve.wait_ge(l1_dve_done, after(b, L1_DVE, ("ffn", g)))
                    dve.tensor_tensor(mod[:, hs_(g)], upd[:, hs_(g)], ynT[:, hs_(g)], ALU.add).then_inc(mod_ready, 1)
                dve.wait_ge(l1_act_done, after(b, L1_ACT, ("B", 1)))
                for gr in range(NGRP):
                    for g in range(2):
                        bank = full1(b, ("xs", gr, g))
                        dve.tensor_tensor(bank[:], bank[:], Bt[:, hs_(g)], ALU.mult).then_inc(u_ready, 1)
                    if gr >= 2:
                        dve.wait_ge(p_ready, b * NGRP + (gr - 1) + CREDIT)
                    else:
                        dve.wait_ge(p_ready, b * NGRP + CREDIT)
                    for g in range(2):
                        bank = bank1d[L1_DVE.index(("xs", gr, g)) % 2]
                        dve.wait_ge(u_ready, b * 2 * NGRP + (2 * gr + g + 1) + CREDIT)
                        h = hs[:, gr % 2, :]
                        if g == 1:
                            dve.wait_ge(l1_dve_done, after(b, L1_DVE, ("xs", gr, 0)))
                        dve.tensor_tensor_scan(h[:, hs_(g)], decay[:, gr:gr + 1].broadcast_to([P, HALF]), bank[:],
                                               0.0 if g == 0 else h[:, HALF - 1:HALF],
                                               ALU.mult, ALU.add).then_inc(l1_dve_done, 1)
                for g in range(2):
                    dve.wait_ge(y_full, b * NGRP + NGRP + CREDIT)
                    dve.scalar_tensor_tensor(yd[:, hs_(g)], xc[:, hs_(g)], scale("D"), ybank[g][:],
                                             ALU.mult, ALU.add).then_inc(yd_ready, 1)
                    dve.wait_ge(yd_ready, b * 2 + (g + 1) + CREDIT)
                    dve.tensor_tensor(yg[:, hs_(g)], yd[:, hs_(g)], gate[:, hs_(g)], ALU.mult).then_inc(yg_ready, 1)
                for g in range(2):
                    bank = full1(b, ("out", g))
                    dve.wait_ge(g1_ready, b * 2 + (g + 1) + CREDIT)
                    dve.wait_ge(stored, b * 32 + CREDIT)
                    dve.scalar_tensor_tensor(t1[:, hs_(g)], bank[:], scale("b_out"), g1[:, hs_(g)],
                                             ALU.add, ALU.mult).then_inc(l1_dve_done, 1)
                    dve.wait_ge(l1_dve_done, after(b, L1_DVE, ("out", g)))
                    dve.tensor_tensor(o[:, hs_(g)], t1[:, hs_(g)], x1[:, hs_(g)], ALU.add).then_inc(o_ready, 1)


def constants():
    i = np.arange(P)
    diff = i[None, :] - i[:, None]
    decay_mask = np.where(diff >= 0, GAMMA ** np.maximum(diff, 0), 0.0)
    gamma_row = np.broadcast_to(GAMMA ** (i + 1.0), (P, P))
    before_mask = (i[:, None] < i[None, :]).astype(np.float32)
    n, dd = i // DPG, i % DPG
    spread = np.zeros((P, NGRP, P), np.float32)
    for g in range(NGRP):
        spread[DPG * g + dd, g, i] = 1.0
    gather = np.zeros((P, 2 * P - DPG), np.float32)
    gather[i, P - DPG + dd] = 1.0
    return {"decay_mask": decay_mask.astype(np.float32), "gamma_row": gamma_row.astype(np.float32),
            "identity": np.eye(P, dtype=np.float32), "before_mask": before_mask,
            "spread": spread, "gather": gather,
            "gamma_col": (GAMMA ** (P - 1.0 - i)).astype(np.float32)[:, None]}


def kernel(**inputs):
    import concourse.bacc as bacc
    from concourse.bass_utils import run_bass_kernel_spmd

    a = {k: np.asarray(v) for k, v in inputs.items()}
    c = constants()
    x = a["L0_attn_x"]

    def columns(v):
        return v.reshape(-1, P).T

    def k_tiles(w):
        return w.reshape(-1, P, w.shape[1]).transpose(1, 0, 2)

    a_log = a["L1_attn_A_log"].reshape(NGRP, DPG, NSTATE).transpose(2, 1, 0).reshape(P, NGRP)
    w_x, b_x = a["L1_attn_W_x"], a["L1_attn_b_x"]
    cols = {"w1_s": columns(a["L0_ffn_w1_s"]), "w2_s": columns(a["L0_ffn_w2_s"]), "h1_s": columns(a["L0_ffn_h1_s"]),
            "h2_s": columns(a["L0_ffn_h2_s"]), "w3_s": columns(a["L0_ffn_w3_s"]), "theta": columns(a["L0_attn_theta"]),
            "b_in": columns(a["L1_attn_b_in"]), "conv_w": a["L1_attn_conv_w"], "conv_b": columns(a["L1_attn_conv_b"]),
            "D": columns(a["L1_attn_D_param"]), "b_out": columns(a["L1_attn_b_out"]), "b1": columns(a["L1_ffn_b1"]),
            "b2": columns(a["L1_ffn_b2"]), "b_x": np.repeat(b_x, DPG).reshape(2, P).T, "A_log": a_log,
            "gamma_col": c.pop("gamma_col")}
    arrays = {
        "x_tok": x.reshape(BATCH, CH, P, P).transpose(0, 2, 1, 3),
        "x_feat": x.transpose(0, 2, 1),
        "small": np.concatenate([cols[k] for k in COLS], axis=1),
        "w_in0": np.stack([a["L0_ffn_w1_w"].T, a["L0_ffn_w2_w"].T], axis=1),
        "h_w": np.stack([k_tiles(a["L0_ffn_h1_w"].T), k_tiles(a["L0_ffn_h2_w"].T)], axis=1),
        "w3T": k_tiles(a["L0_ffn_w3_w"].T),
        "retention_w": np.stack([a["L0_attn_weight_q"].T, a["L0_attn_weight_k"].T, a["L0_attn_weight_v"]], axis=1),
        "l1_w": np.concatenate([a["L1_attn_W_in"], np.repeat(w_x, DPG, axis=1),
                                np.repeat(a["L1_ffn_w_router"][:, None], P, axis=1), a["L1_attn_W_out"],
                                a["L1_ffn_W1"]], axis=1),
        "w2_l1": k_tiles(a["L1_ffn_W2"]),
        **c,
    }
    nc = bacc.Bacc("TRN2", target_bir_lowering=False, num_devices=1)
    aps = {}
    for name, value in arrays.items():
        arrays[name] = np.ascontiguousarray(value)
        aps[name] = nc.dram_tensor(name, arrays[name].shape, mybir.dt.from_np(arrays[name].dtype),
                                   kind="ExternalInput").ap()
    out = nc.dram_tensor("out", (BATCH, P, SEQ), F32, kind="ExternalOutput").ap()
    program(nc, out=out, **aps)
    got = run_bass_kernel_spmd(nc, [arrays], core_ids=[0]).results[0]["out"]
    return np.ascontiguousarray(got.transpose(0, 2, 1))
```

```python
from contextlib import ExitStack

import numpy as np

import concourse.bass as bass
from concourse import mybir

F32 = mybir.dt.float32
F32R = mybir.dt.float32r
BF16 = mybir.dt.bfloat16
I32 = mybir.dt.int32
ALU = mybir.AluOpType
ACT = mybir.ActivationFunctionType

P = 128
BATCH = 4
SEQ = 1024
HALF = 512
CH = SEQ // P
CPH = HALF // P
HID = 512
KT = HID // P
NSTATE = 16
DPG = P // NSTATE
NGRP = P // DPG
TAPS = 4
CREDIT = 1
MEM_STEPS = CH - 3
TOPK = SEQ // 2
GAMMA = 0.96875
EPS = 1e-5

COLS = {}
_at = 0
for _name, _n in [("w1_s", KT), ("w2_s", KT), ("h1_s", KT), ("h2_s", KT), ("w3_s", 1), ("theta", 1),
                  ("b_in", 2), ("conv_w", TAPS), ("conv_b", 1), ("D", 1), ("b_out", 1), ("b1", KT),
                  ("b2", 1), ("b_x", 2), ("A_log", NGRP), ("gamma_col", 1)]:
    COLS[_name] = slice(_at, _at + _n)
    _at += _n
NCOLS = _at

L0_ACT = ([("xnT", g) for g in range(2)] + [("q", g) for g in range(2)]
          + [("z1", 0, m) for m in range(KT)] + [("u", g) for g in range(2)]
          + [("h1", 0, m) for m in range(KT)] + [("h2", 0, m) for m in range(KT)] + [("w3", 0)]
          + [("z1", 1, m) for m in range(KT)]
          + [("h1", 1, m) for m in range(KT)] + [("h2", 1, m) for m in range(KT)] + [("w3", 1)])
L0_DVE = ([(k, g) for g in range(2) for k in ("scores", "outer")]
          + [("z2", 0, m) for m in range(KT)] + [("s", 0)] + [("z2", 1, m) for m in range(KT)] + [("s", 1)])
L1_ACT = ([(k, g) for k in ("xnT", "ssm", "score", "gate", "B", "C") for g in range(2)]
          + [("ffn", g, m) for g in range(2) for m in range(KT)])
L1_DVE = ([(k, g) for k in ("tok", "score_col", "rank") for g in range(2)]
          + [("xs", 0, g) for g in range(2)] + [("ffn", g) for g in range(2)]
          + [("xs", gr, g) for gr in range(1, NGRP) for g in range(2)] + [("out", g) for g in range(2)])
HIDDEN = [(k, g, m) for g in range(2) for k in ("z", "h1", "h2") for m in range(KT)]
NPLAIN = 3


def after(b, order, job):
    return b * len(order) + (order.index(job) + 1 + CREDIT)


def program(nc, x_tok, x_feat, small, w_in0, h_w, w3T, retention_w, l1_w, w2_l1, decay_mask, gamma_row,
            identity, before_mask, spread, gather, out):
    with ExitStack() as ctx:
        def sb(name, shape, dt=F32):
            return ctx.enter_context(nc.sbuf_tensor(name, shape, dt))

        def ps(name, shape, dt=F32):
            return ctx.enter_context(nc.psum_tensor(name, shape, dt))

        def sem(name):
            return ctx.enter_context(nc.semaphore(name))

        col = sb("col", [P, NCOLS])
        w12h = sb("w12h", [P, 2, HID], F32R)
        w12l = sb("w12l", [P, 2, HID], F32R)
        hTh = sb("hTh", [P, 2, KT, HID], F32R)
        hTl = sb("hTl", [P, 2, KT, HID], F32R)
        w3h = sb("w3h", [P, KT, P], F32R)
        w3l = sb("w3l", [P, KT, P], F32R)
        rw = sb("rw", [P, 3, P])
        lw = sb("lw", [P, 6 * P + HID])
        w2l = sb("w2l", [P, KT, P])
        mask = sb("mask", [P, P])
        grow = sb("grow", [P, P])
        ident = sb("ident", [P, P])
        tri = sb("tri", [P, P])
        spr = sb("spr", [P, NGRP // 2, P], F32R)
        gat = sb("gat", [P, 2 * P - DPG])
        ones = sb("ones", [P, P], BF16)
        half_neg = sb("half_neg", [P, CH])
        eps = sb("eps", [P, CH])
        wait_carrier = sb("wait_carrier", [P, 1])
        theta1 = sb("theta1", [P, 1])
        wk_th = sb("wk_th", [P, P])
        qk = sb("qk", [P, P])
        aexp = sb("aexp", [P, NGRP])
        decay = sb("decay", [P, NGRP])
        inexact = sb("inexact", [P, 4])
        inexact_b = sb("inexact_b", [P, 4], BF16)
        inexact_i = sb("inexact_i", [P, 1], I32)
        W_IN, W_B, W_C, W_R, W_OUT, W_1 = (lw[:, 0:2 * P], lw[:, 2 * P:3 * P], lw[:, 3 * P:4 * P],
                                           lw[:, 4 * P:5 * P], lw[:, 5 * P:6 * P], lw[:, 6 * P:])

        xt = sb("xt", [P, CH, P])
        xg = xt
        xf = sb("xf", [P, SEQ])
        st0 = sb("st0", [P, CH, 6])
        mv0 = sb("mv0", [P, CH, 2])
        ve0 = sb("ve0", [P, CH])
        rstd0 = sb("rstd0", [P, CH])
        xn = sb("xn", [P, CH, P])
        xnT = sb("xnT", [P, SEQ])
        xnTh = sb("xnTh", [P, SEQ], F32R)
        xnTl = sb("xnTl", [P, SEQ], F32R)
        q = sb("q", [P, SEQ])
        qg = q
        u = q
        sc = sb("sc", [P, CH, P])
        g0 = sc[:].rearrange("p c i -> p (c i)")
        mem = sb("mem", [P, CH, P])
        silu1 = sb("silu1", [P, 2, HALF])
        plain = sb("plain", [P, NPLAIN, HALF])
        hidAh = sb("hidAh", [P, KT, HALF], F32R)
        hidAl = sb("hidAl", [P, KT, HALF], F32R)
        hidBh = sb("hidBh", [P, KT, HALF], F32R)
        hidBl = sb("hidBl", [P, KT, HALF], F32R)
        pair = {"z": (hidAh, hidAl), "h1": (hidBh, hidBl), "h2": (hidAh, hidAl)}
        x1 = sb("x1", [P, SEQ])
        sg = x1

        res = sb("res", [P, SEQ])
        st1 = sb("st1", [P, CH, 6])
        mv1 = sb("mv1", [P, CH, 2])
        ve1 = sb("ve1", [P, CH])
        rstd1 = sb("rstd1", [P, CH])
        early = sb("early", [P, 2 * SEQ])
        yn = early[:, 0:SEQ].rearrange("p (c d) -> p c d", d=P)
        tie = yn
        beats = early[:, SEQ:2 * SEQ].bitcast(BF16).rearrange("p (a t) -> p a t", a=2)
        fh = early[:].rearrange("p (k t) -> p k t", k=KT)
        ynT = sb("ynT", [P, SEQ])
        srow = sb("srow", [P, SEQ])
        o = srow
        scol = sb("scol", [P, CH])
        hs = sb("hs", [P, 2, SEQ])
        ssm = hs[:].rearrange("p a t -> p (a t)")[:, 0:TAPS - 1 + SEQ]
        xc = sb("xc", [P, SEQ])
        xpair = sb("xpair", [P, 2, SEQ], F32R)
        Bt = sb("Bt", [P, SEQ])
        yg = Bt
        cv = [Bt, xc]
        Ct = sb("Ct", [P, SEQ])
        gate = xnT
        g1 = sb("g1", [P, SEQ])
        pr = sb("pr", [P, 2, SEQ])

        bank0a = [ps(f"bank0a{i}", [P, HALF]) for i in range(2)]
        bank0d = ps("bank0d", [P, HALF])
        bank1a = ps("bank1a", [P, HALF])
        bank1d = [ps(f"bank1d{i}", [P, HALF]) for i in range(2)]
        ybank = [ps(f"ybank{i}", [P, HALF]) for i in range(2)]

        l0_dve_full = sem("l0_dve_full")
        x_tok_in = sem("x_tok_in")
        x1_ready = sem("x1_ready")
        x_feat_in = sem("x_feat_in")
        o_ready = sem("o_ready")
        stored = sem("stored")
        params = sem("params")
        consts_set = sem("consts_set")
        aggr0 = sem("aggr0")
        eps0 = sem("eps0")
        rstd0_ready = sem("rstd0_ready")
        aggr1 = sem("aggr1")
        eps1 = sem("eps1")
        rstd1_ready = sem("rstd1_ready")
        l0_act_done = sem("l0_act_done")
        xn_low = sem("xn_low")
        qg_ready = sem("qg_ready")
        z_high = sem("z_high")
        hidden_low = sem("hidden_low")
        l1_act_done = sem("l1_act_done")
        y_full = sem("y_full")
        l1_dve_done = sem("l1_dve_done")
        p_ready = sem("p_ready")
        pad_ready = sem("pad_ready")
        l1_params = sem("l1_params")
        theta_ready = sem("theta_ready")
        aexp_ready = sem("aexp_ready")
        decay_ready = sem("decay_ready")
        weight_high = sem("weight_high")
        l0_act_full = sem("l0_act_full")
        l1_act_full = sem("l1_act_full")
        l0_dve_done = sem("l0_dve_done")
        res_ready = sem("res_ready")
        mod_ready = sem("mod_ready")
        yg_ready = sem("yg_ready")
        conv_step = sem("conv_step")
        xc_ready = sem("xc_ready")
        x_high = sem("x_high")
        sig_ready = sem("sig_ready")
        l1_dve_full = sem("l1_dve_full")
        g1_ready = sem("g1_ready")
        spr_ready = sem("spr_ready")
        weight_low = sem("weight_low")
        xn_ready = sem("xn_ready")
        xg_ready = sem("xg_ready")
        beats_ready = sem("beats_ready")
        ranked = sem("ranked")
        yd_ready = sem("yd_ready")
        x_low = sem("x_low")
        wk_ready = sem("wk_ready")
        qk_full = sem("qk_full")
        qk_ready = sem("qk_ready")
        inexact_ready = sem("inexact_ready")
        inexact_full = sem("inexact_full")
        inexact_known = sem("inexact_known")
        stats0 = sem("stats0")
        mem_step = sem("mem_step")
        stats1 = sem("stats1")
        tie_ready = sem("tie_ready")
        sigh_ready = sem("sigh_ready")
        u_ready = sem("u_ready")
        inexact_step = sem("inexact_step")
        raw_loaded = [sem(f"raw_loaded{i}") for i in range(4)]
        NPARAM = 5
        NPARAM_L1 = 5

        hs_ = lambda g: slice(g * HALF, (g + 1) * HALF)
        ck = lambda c: slice(c * P, (c + 1) * P)

        def scale(name, m=0):
            s = COLS[name].start + m
            return col[:, s:s + 1]

        raw_h = [hs[:].rearrange("p a t -> p (a t)"), pr[:].rearrange("p a t -> p (a t)")]
        raw_w12, raw_w3 = Bt[:], Ct[:, 0:KT * P]
        raw_spr = g1[:, 0:NGRP // 2 * P]
        FFN_WEIGHTS = [(raw_w12, w12h[:].rearrange("p a n -> p (a n)"), w12l[:].rearrange("p a n -> p (a n)"))]
        for i in range(2):
            FFN_WEIGHTS.append((raw_h[i], hTh[:, i].rearrange("p k n -> p (k n)"),
                                hTl[:, i].rearrange("p k n -> p (k n)")))
        FFN_WEIGHTS.append((raw_w3, w3h[:].rearrange("p k n -> p (k n)"), w3l[:].rearrange("p k n -> p (k n)")))

        block = ctx.enter_context(nc.Block())

        @block.sync
        def _(sp):
            def load_x(b):
                sp.wait_ge(l0_dve_full, (b - 1) * len(L0_DVE) + (L0_DVE.index(("outer", 1)) + 1 + CREDIT))
                sp.dma_start(xt[:], x_tok[bass.ds(b, 1)].rearrange("o p c d -> (o p) c d")).then_inc(x_tok_in, 16)
                sp.wait_ge(x1_ready, b * 2 + CREDIT)
                sp.dma_start(xf[:], x_feat[bass.ds(b, 1)].rearrange("o p t -> (o p) t")).then_inc(x_feat_in, 16)

            def store(b):
                for g in range(2):
                    sp.wait_ge(o_ready, b * 2 + (g + 1) + CREDIT)
                    sp.dma_start(out[bass.ds(b, 1), :, hs_(g)].rearrange("o p t -> (o p) t"), o[:, hs_(g)]).then_inc(stored, 16)

            sp.dma_start(xt[:], x_tok[0]).then_inc(x_tok_in, 16)
            sp.dma_start(ident[:], identity).then_inc(params, 16)
            sp.dma_start(col[:], small).then_inc(params, 16)
            sp.dma_start(rw[:], retention_w).then_inc(params, 16)
            sp.dma_start(raw_w12, w_in0).then_inc(raw_loaded[0], 16)
            for i in range(2):
                sp.dma_start(raw_h[i], h_w[:, i]).then_inc(raw_loaded[1 + i], 16)
            sp.dma_start(raw_w3, w3T).then_inc(raw_loaded[3], 16)
            sp.dma_start(xf[:], x_feat[0]).then_inc(x_feat_in, 16)
            sp.sem_inc(stored, CREDIT)
            with sp.Fori(0, BATCH - 1) as b:
                load_x(b + 1)
                store(b)
            store(BATCH - 1)
            sp.wait_ge(stored, BATCH * 2 * 16 + CREDIT)

        @block.gpsimd
        def _(pool):
            pool.memset(eps[:], EPS).then_inc(consts_set, 1)
            pool.memset(half_neg[:], -0.5).then_inc(consts_set, 1)
            pool.memset(mem[:, 0, :], 0.0).then_inc(consts_set, 1)
            pool.memset(ones[:], 1.0).then_inc(consts_set, 1)

            def rstd_l0(b):
                pool.wait_ge(aggr0, b + 1 + CREDIT)
                pool.tensor_tensor(ve0[:], mv0[:, :, 1], eps[:], ALU.add).then_inc(eps0, 1)
                pool.wait_ge(eps0, b + 1 + CREDIT)
                pool.tensor_tensor(rstd0[:], ve0[:], half_neg[:], ALU.pow).then_inc(rstd0_ready, 1)

            def rstd_l1(b):
                for g in range(2):
                    c = slice(g * CPH, (g + 1) * CPH)
                    pool.wait_ge(aggr1, b * 2 + (g + 1) + CREDIT)
                    pool.tensor_tensor(ve1[:, c], mv1[:, c, 1], eps[:, c], ALU.add).then_inc(eps1, 1)
                    pool.wait_ge(eps1, b * 2 + (g + 1) + CREDIT)
                    pool.tensor_tensor(rstd1[:, c], ve1[:, c], half_neg[:, c], ALU.pow).then_inc(rstd1_ready, 1)

            def low_xn(b, g):
                pool.wait_ge(l0_act_done, after(b, L0_ACT, ("xnT", g)))
                pool.tensor_tensor(xnTl[:, hs_(g)], xnT[:, hs_(g)], xnTh[:, hs_(g)].bitcast(F32),
                                   ALU.subtract).then_inc(xn_low, 1)

            def scale_q(b, g):
                pool.wait_ge(l0_dve_full, after(b, L0_DVE, ("scores", g)))
                v = lambda t: t[:, hs_(g)].rearrange("p (c i) -> p c i", i=P)
                pool.tensor_tensor(v(qg), v(q), grow[:].rearrange("p (o i) -> p o i", o=1).broadcast_to([P, CPH, P]),
                                   ALU.mult).then_inc(qg_ready, 1)

            def low_hidden(b, kind, g, m):
                k = HIDDEN.index((kind, g, m))
                if kind == "z":
                    pool.wait_ge(z_high, b * 2 * KT + (g * KT + m + 1) + CREDIT)
                else:
                    pool.wait_ge(l0_act_done, after(b, L0_ACT, (kind, g, m)))
                high, low = pair[kind]
                pool.tensor_tensor(low[:, m, :], plain[:, k % NPLAIN, :], high[:, m, :].bitcast(F32),
                                   ALU.subtract).then_inc(hidden_low, 1)

            def weigh_states(b, gr):
                if gr == 0:
                    pool.wait_ge(l1_act_done, after(b, L1_ACT, ("C", 1)))
                    pool.wait_ge(y_full, b * NGRP + CREDIT)
                pool.wait_ge(l1_dve_done, after(b, L1_DVE, ("xs", gr, 1)))
                if gr >= 2:
                    pool.wait_ge(y_full, b * NGRP + (gr - 1) + CREDIT)
                pool.tensor_tensor(pr[:, gr % 2, :], hs[:, gr % 2, :], Ct[:], ALU.mult).then_inc(p_ready, 1)

            def before_states(b0, b1):
                if b0 is not None:
                    rstd_l0(b0)
                if b1 is not None:
                    rstd_l1(b1)
                if b0 is not None:
                    for g in range(2):
                        low_xn(b0, g)
                    for g in range(2):
                        scale_q(b0, g)
                    for m in range(KT):
                        low_hidden(b0, "z", 0, m)
                    for m in range(KT):
                        low_hidden(b0, "h1", 0, m)

            def slot(b0, b1, k):
                if b1 is not None:
                    weigh_states(b1, k)
                if b0 is not None:
                    if k < 4:
                        low_hidden(b0, "h2", 0, k)
                    elif k in (5, 6):
                        for m in (2 * (k - 5), 2 * (k - 5) + 1):
                            low_hidden(b0, "z", 1, m)
                    elif 7 <= k < 11:
                        low_hidden(b0, "h1", 1, k - 7)
                    elif 11 <= k < 15:
                        low_hidden(b0, "h2", 1, k - 11)

            def stage(b0, b1):
                before_states(b0, b1)
                for k in range(NGRP):
                    slot(b0, b1, k)

            pool.wait_ge(consts_set, 4)
            for semaphore in (eps0, rstd0_ready, qg_ready, eps1, rstd1_ready, p_ready, xn_low, hidden_low):
                pool.sem_inc(semaphore, CREDIT)
            stage(0, None)
            with pool.Fori(0, BATCH - 1) as b:
                stage(b + 1, b)
            stage(None, BATCH - 1)

        @block.scalar
        def _(act):
            act.dma_start(mask[:], decay_mask).then_inc(params, 16)
            act.dma_start(grow[:], gamma_row).then_inc(params, 16)
            for dst, src in ((raw_spr, spread), (lw[:], l1_w), (gat[:], gather), (tri[:], before_mask), (w2l[:], w2_l1)):
                act.dma_start(dst, src).then_inc(l1_params, 16)
            for semaphore in (l0_act_done, l1_act_done, xc_ready, sig_ready, g1_ready, z_high, res_ready, x_high):
                act.sem_inc(semaphore, CREDIT)
            act.wait_ge(params, 16 * NPARAM)
            act.activation(theta1[:], col[:, COLS["theta"]], ACT.Exp, scale=0.0).then_inc(theta_ready, 1)
            act.activation(aexp[:], col[:, COLS["A_log"]], ACT.Exp).then_inc(aexp_ready, 1)
            act.wait_ge(aexp_ready, 1)
            act.activation(decay[:], aexp[:], ACT.Exp, scale=-1.0).then_inc(decay_ready, 1)
            for i in (0, 1, 2, 3):
                raw, high, _ = FFN_WEIGHTS[i]
                act.wait_ge(raw_loaded[i], 16)
                act.activation(high, raw, ACT.Copy).then_inc(weight_high, 1)

            def full0(b, job):
                act.wait_ge(l0_act_full, after(b, L0_ACT, job))
                return bank0a[L0_ACT.index(job) % 2]

            def take1(b, job, out_ap, func=ACT.Copy, **kw):
                act.wait_ge(l1_act_full, after(b, L1_ACT, job))
                act.activation(out_ap, bank1a[:], func, **kw).then_inc(l1_act_done, 1)

            def plain_free(eng, b, k):
                if k >= NPLAIN:
                    eng.wait_ge(hidden_low, b * len(HIDDEN) + (k - NPLAIN + 1) + CREDIT)
                else:
                    eng.wait_ge(hidden_low, b * len(HIDDEN) + CREDIT)

            def hidden(b, kind, g, m):
                k = HIDDEN.index((kind, g, m))
                plain_free(act, b, k)
                bank = full0(b, (kind, g, m))
                act.activation(plain[:, k % NPLAIN, :], bank[:], ACT.Gelu, scale=scale(kind + "_s", m))
                act.activation(pair[kind][0][:, m, :], bank[:], ACT.Gelu,
                               scale=scale(kind + "_s", m)).then_inc(l0_act_done, 1)

            def z_silu(b, g, m):
                if m >= 2:
                    act.wait_ge(l0_dve_done, after(b, L0_DVE, ("z2", g, m - 2)))
                elif g == 1:
                    act.wait_ge(l0_dve_done, after(b, L0_DVE, ("z2", 0, m + 2)))
                else:
                    act.wait_ge(l0_dve_done, b * len(L0_DVE) + CREDIT)
                bank = full0(b, ("z1", g, m))
                act.activation(silu1[:, m % 2, :], bank[:], ACT.Silu, scale=scale("w1_s", m)).then_inc(l0_act_done, 1)

            def z_round(b, g, m):
                k = HIDDEN.index(("z", g, m))
                act.wait_ge(l0_dve_done, after(b, L0_DVE, ("z2", g, m)))
                act.activation(hidAh[:, m, :], plain[:, k % NPLAIN, :], ACT.Copy).then_inc(z_high, 1)

            def gate_l0(b, g):
                bank = full0(b, ("w3", g))
                act.activation(g0[:, hs_(g)], bank[:], ACT.Silu, scale=scale("w3_s")).then_inc(l0_act_done, 1)

            def before_states(b0, b1):
                if b1 is not None:
                    act.wait_ge(x1_ready, b1 * 2 + (2 + CREDIT))
                    act.wait_ge(o_ready, b1 * 2 + CREDIT)
                    act.activation(res[:], x1[:], ACT.Copy).then_inc(res_ready, 1)
                if b0 is not None:
                    for g in range(2):
                        bank = full0(b0, ("xnT", g))
                        if b1 is not None:
                            act.wait_ge(yg_ready, b1 * 2 + CREDIT)
                        act.activation(xnT[:, hs_(g)], bank[:], ACT.Copy)
                        act.activation(xnTh[:, hs_(g)], bank[:], ACT.Copy).then_inc(l0_act_done, 1)
                    for g in range(2):
                        act.wait_ge(l0_dve_full, b0 * len(L0_DVE) + CREDIT)
                        bank = full0(b0, ("q", g))
                        act.activation(q[:, hs_(g)], bank[:], ACT.Copy).then_inc(l0_act_done, 1)
                if b1 is not None:
                    for g in range(2):
                        act.wait_ge(mod_ready, b1 * 2 + CREDIT)
                        take1(b1, ("xnT", g), ynT[:, hs_(g)])
                    for g in range(2):
                        act.wait_ge(p_ready, b1 * NGRP + CREDIT)
                        take1(b1, ("ssm", g), ssm[:, TAPS - 1 + g * HALF:TAPS - 1 + (g + 1) * HALF], ACT.Identity,
                              bias=scale("b_in"))
                    for g in range(2):
                        act.wait_ge(stored, b1 * 32 + CREDIT)
                        take1(b1, ("score", g), srow[:, hs_(g)])
                if b0 is not None:
                    z_silu(b0, 0, 0)
                    for m in range(1, KT):
                        z_silu(b0, 0, m)
                        z_round(b0, 0, m - 1)
                    z_round(b0, 0, KT - 1)
                if b1 is not None:
                    for g in range(2):
                        act.wait_ge(yg_ready, b1 * 2 + CREDIT)
                        take1(b1, ("gate", g), gate[:, hs_(g)], ACT.Silu, bias=scale("b_in", 1))
                if b0 is not None:
                    for g in range(2):
                        bank = full0(b0, ("u", g))
                        act.activation(u[:, hs_(g)], bank[:], ACT.Copy).then_inc(l0_act_done, 1)
                if b1 is not None:
                    act.wait_ge(conv_step, b1 * TAPS + TAPS + CREDIT)
                    act.activation(xc[:], cv[(TAPS - 1) % 2][:], ACT.Silu, bias=scale("conv_b")).then_inc(xc_ready, 1)
                    act.wait_ge(xc_ready, b1 + 1 + CREDIT)
                    for half in range(2):
                        rows = slice(half * P // 2, (half + 1) * P // 2)
                        last = act.activation(xpair[rows, half, :], xc[rows, :], ACT.Copy)
                    last.then_inc(x_high, 1)
                if b0 is not None:
                    for m in range(KT):
                        hidden(b0, "h1", 0, m)
                if b1 is not None:
                    for g in range(2):
                        take1(b1, ("B", g), Bt[:, hs_(g)], ACT.Identity, bias=scale("b_x"))
                    for g in range(2):
                        take1(b1, ("C", g), Ct[:, hs_(g)], ACT.Identity, bias=scale("b_x", 1))
                    act.activation(g1[:], srow[:], ACT.Tanh, scale=0.5).then_inc(sig_ready, 1)
                    for g in range(2):
                        if g == 0:
                            act.wait_ge(l1_dve_full, b1 * len(L1_DVE) + CREDIT)
                        else:
                            act.wait_ge(l1_dve_full, after(b1, L1_DVE, ("ffn", 0)))
                        for m in range(KT):
                            take1(b1, ("ffn", g, m), fh[:, m, :], ACT.Gelu_apprx_tanh, bias=scale("b1", m))

            def slot(b0, b1, k):
                if b0 is not None:
                    if k < 4:
                        hidden(b0, "h2", 0, k)
                    elif k == 4:
                        if b1 is not None:
                            for g in range(2):
                                act.wait_ge(mod_ready, b1 * 2 + (g + 1) + CREDIT)
                                act.activation(g1[:, hs_(g)], g1[:, hs_(g)], ACT.Silu).then_inc(g1_ready, 1)
                        act.wait_ge(x1_ready, b0 * 2 + CREDIT)
                        gate_l0(b0, 0)
                        z_silu(b0, 1, 0)
                    elif k == 5:
                        for m in (1, 2):
                            z_silu(b0, 1, m)
                            z_round(b0, 1, m - 1)
                    elif k == 6:
                        z_silu(b0, 1, 3)
                        z_round(b0, 1, 2)
                        z_round(b0, 1, 3)
                    elif 7 <= k < 11:
                        hidden(b0, "h1", 1, k - 7)
                    elif 11 <= k < 15:
                        hidden(b0, "h2", 1, k - 11)
                    else:
                        gate_l0(b0, 1)
                elif k == 4:
                    for g in range(2):
                        act.wait_ge(mod_ready, b1 * 2 + (g + 1) + CREDIT)
                        act.activation(g1[:, hs_(g)], g1[:, hs_(g)], ACT.Silu).then_inc(g1_ready, 1)

            def stage(b0, b1):
                before_states(b0, b1)
                for k in range(NGRP):
                    slot(b0, b1, k)

            stage(0, None)
            act.wait_ge(l1_params, 16 * NPARAM_L1)
            act.activation(spr[:].rearrange("p k n -> p (k n)"), raw_spr, ACT.Copy).then_inc(spr_ready, 1)
            act.wait_ge(weight_low, len(FFN_WEIGHTS))
            act.wait_ge(spr_ready, 1)
            with act.Fori(0, BATCH - 1) as b:
                stage(b + 1, b)
            stage(None, BATCH - 1)

        @block.tensor
        def _(pe):
            def open0a(b, job):
                i = L0_ACT.index(job)
                pe.wait_ge(l0_act_done, b * len(L0_ACT) + (max(i - 1, 0) + CREDIT))
                return bank0a[i % 2]

            def open0d(b, job):
                pe.wait_ge(l0_dve_done, b * len(L0_DVE) + (L0_DVE.index(job) + CREDIT))
                return bank0d

            def open1a(b, job):
                pe.wait_ge(l1_act_done, b * len(L1_ACT) + (L1_ACT.index(job) + CREDIT))
                return bank1a

            def open1d(b, job):
                i = L1_DVE.index(job)
                pe.wait_ge(l1_dve_done, b * len(L1_DVE) + (max(i - 1, 0) + CREDIT))
                return bank1d[i % 2]

            def retention_in(b):
                for g in range(2):
                    pe.wait_ge(xn_ready, b * 2 + (g + 1) + CREDIT)
                    bank = open0a(b, ("xnT", g))
                    for c in range(CPH):
                        last = pe.transpose(bank[:, ck(c)], xn[:, g * CPH + c, :], ident[:])
                    last.then_inc(l0_act_full, 1)
                for g in range(2):
                    bank = open0a(b, ("q", g))
                    pe.wait_ge(l0_act_done, after(b, L0_ACT, ("xnT", g)))
                    pe.matmul(bank[:], qk[:], xnT[:, hs_(g)], start=True, stop=True).then_inc(l0_act_full, 1)

            def retention_chunks(b):
                pe.wait_ge(xg_ready, b + 1 + CREDIT)
                for g in range(2):
                    bank = open0d(b, ("scores", g))
                    pe.wait_ge(l0_act_done, after(b, L0_ACT, ("q", g)))
                    for c in range(g * CPH, (g + 1) * CPH):
                        last = pe.matmul(bank[:, ck(c - g * CPH)], xnT[:, ck(c)], q[:, ck(c)], start=True, stop=True)
                    last.then_inc(l0_dve_full, 1)
                    bank = open0d(b, ("outer", g))
                    for c in range(g * CPH, (g + 1) * CPH):
                        last = pe.matmul(bank[:, ck(c - g * CPH)], xg[:, c, :], xn[:, c, :], start=True, stop=True)
                    last.then_inc(l0_dve_full, 1)

            def retention_out(b):
                for g in range(2):
                    bank = open0a(b, ("u", g))
                    pe.wait_ge(qg_ready, b * 2 + (g + 1) + CREDIT)
                    pe.wait_ge(l0_dve_done, after(b, L0_DVE, ("outer", g)))
                    for c in range(g * CPH, (g + 1) * CPH):
                        pe.matmul(bank[:, ck(c - g * CPH)], xn[:, c, :], sc[:, c, :], start=True, stop=False)
                        last = pe.matmul(bank[:, ck(c - g * CPH)], mem[:, c, :], qg[:, ck(c)], start=False, stop=True)
                    last.then_inc(l0_act_full, 1)

            def value(b, g):
                bank = open0d(b, ("s", g))
                pe.wait_ge(l0_act_done, after(b, L0_ACT, ("u", g)))
                pe.matmul(bank[:], rw[:, 2, :], u[:, hs_(g)], start=True, stop=True).then_inc(l0_dve_full, 1)

            def rest(exact):
                def split_product(bank, terms):
                    passes = []
                    for wh, wl, xh, xl in terms:
                        passes += [(wh, xh), (wh, xl)] if exact else [(wh, xh), (wh, xl), (wl, xh)]
                    for n, (w, x) in enumerate(passes):
                        last = pe.matmul(bank[:], w, x, start=(n == 0), stop=(n == len(passes) - 1))
                    return last

                def ffn_in(b, g, m):
                    x = (xnTh[:, hs_(g)], xnTl[:, hs_(g)])
                    pe.wait_ge(xn_low, b * 2 + (g + 1) + CREDIT)
                    bank = open0a(b, ("z1", g, m))
                    split_product(bank, [(w12h[:, 0, ck(m)], w12l[:, 0, ck(m)], *x)]).then_inc(l0_act_full, 1)
                    bank = open0d(b, ("z2", g, m))
                    split_product(bank, [(w12h[:, 1, ck(m)], w12l[:, 1, ck(m)], *x)]).then_inc(l0_dve_full, 1)

                def hidden_ready(b, kind, g):
                    pe.wait_ge(hidden_low, b * len(HIDDEN) + (HIDDEN.index((kind, g, KT - 1)) + 1 + CREDIT))

                def hidden(b, kind, g, m):
                    i = ("h1", "h2").index(kind)
                    source = ("z", "h1")[i]
                    bank = open0a(b, (kind, g, m))
                    hidden_ready(b, source, g)
                    high, low = pair[source]
                    split_product(bank, [(hTh[:, i, kt, ck(m)], hTl[:, i, kt, ck(m)], high[:, kt, :], low[:, kt, :])
                                         for kt in range(KT)]).then_inc(l0_act_full, 1)

                def ffn_out(b, g):
                    bank = open0a(b, ("w3", g))
                    hidden_ready(b, "h2", g)
                    split_product(bank, [(w3h[:, kt, :], w3l[:, kt, :], hidAh[:, kt, :], hidAl[:, kt, :])
                                         for kt in range(KT)]).then_inc(l0_act_full, 1)

                def project(b, job, g, w, source=ynT):
                    bank = open1a(b, (job, g))
                    pe.matmul(bank[:], w, source[:, hs_(g)], start=True, stop=True).then_inc(l1_act_full, 1)

                def to_tokens(b):
                    for g in range(2):
                        bank = open1d(b, ("tok", g))
                        pe.wait_ge(x1_ready, b * 2 + (g + 1) + CREDIT)
                        for c in range(CPH):
                            last = pe.transpose(bank[:, ck(c)], x1[:, ck(g * CPH + c)], ident[:])
                        last.then_inc(l1_dve_full, 1)

                def norm_to_features(b):
                    for g in range(2):
                        bank = open1a(b, ("xnT", g))
                        pe.wait_ge(l1_dve_done, after(b, L1_DVE, ("tok", g)))
                        for c in range(CPH):
                            last = pe.transpose(bank[:, ck(c)], yn[:, g * CPH + c, :], ident[:])
                        last.then_inc(l1_act_full, 1)

                def score_columns(b):
                    for g in range(2):
                        bank = open1d(b, ("score_col", g))
                        pe.wait_ge(l1_act_done, after(b, L1_ACT, ("score", g)))
                        for c in range(CPH):
                            last = pe.transpose(bank[:, ck(c)], srow[:, ck(g * CPH + c)], ident[:])
                        last.then_inc(l1_dve_full, 1)

                def rank(b, c, banks):
                    pe.wait_ge(beats_ready, b * CH + (c + 1) + CREDIT)
                    for g in range(2):
                        last = pe.matmul(banks[g][:], ones[:], beats[:, c % 2, hs_(g)],
                                         start=(c == 0), stop=(c == CH - 1))
                        if c == CH - 1:
                            last.then_inc(l1_dve_full, 1)
                    if c < CH - 1:
                        last.then_inc(ranked, 1)

                def mod_ffn(b, g):
                    for m in range(KT):
                        bank = open1a(b, ("ffn", g, m))
                        pe.matmul(bank[:], W_1[:, ck(m)], ynT[:, hs_(g)], start=True, stop=True).then_inc(l1_act_full, 1)
                    bank = open1d(b, ("ffn", g))
                    pe.wait_ge(l1_act_done, after(b, L1_ACT, ("ffn", g, KT - 1)))
                    for kt in range(KT):
                        last = pe.matmul(bank[:], w2l[:, kt, :], fh[:, kt, :], start=(kt == 0), stop=(kt == KT - 1))
                    last.then_inc(l1_dve_full, 1)

                def spread_x(b, gr):
                    half, k = divmod(gr, NGRP // 2)
                    for g in range(2):
                        bank = open1d(b, ("xs", gr, g))
                        pe.matmul(bank[:], spr[:, k, :], xpair[:, half, hs_(g)], start=True, stop=True).then_inc(l1_dve_full, 1)

                def gather_y(b, gr):
                    if gr == 0:
                        pe.wait_ge(yd_ready, b * 2 + CREDIT)
                    pe.wait_ge(p_ready, b * NGRP + (gr + 1) + CREDIT)
                    for g in range(2):
                        last = pe.matmul(ybank[g][:], gat[:, P - DPG * (gr + 1):2 * P - DPG * (gr + 1)],
                                         pr[:, gr % 2, hs_(g)], start=(gr == 0), stop=(gr == NGRP - 1))
                    last.then_inc(y_full, 1)

                def fill(b0, b1, k):
                    if k < KT:
                        if b0 is not None:
                            hidden(b0, "h1", 0, k)
                    elif b1 is not None:
                        if k == KT:
                            pe.wait_ge(xc_ready, b1 + 1 + CREDIT)
                        project(b1, ("B", "B", "C", "C")[k - KT], k % 2, (W_B, W_C)[(k - KT) // 2], xc)

                def before_states(b0, b1, first=False):
                    if b1 is not None:
                        to_tokens(b1)
                    if b0 is not None and not first:
                        retention_in(b0)
                    if b1 is not None:
                        norm_to_features(b1)
                    if b0 is not None and not first:
                        retention_chunks(b0)
                    if b1 is not None:
                        for g in range(2):
                            pe.wait_ge(l1_act_done, after(b1, L1_ACT, ("xnT", g)))
                            project(b1, "ssm", g, W_IN[:, 0:P])
                        for g in range(2):
                            project(b1, "score", g, W_R)
                    if b0 is not None:
                        for m in range(KT):
                            ffn_in(b0, 0, m)
                    if b1 is not None:
                        score_columns(b1)
                        for g in range(2):
                            project(b1, "gate", g, W_IN[:, P:2 * P])
                    if b0 is not None:
                        retention_out(b0)
                    if b1 is not None:
                        banks = [open1d(b1, ("rank", g)) for g in range(2)]
                    for c in range(CH):
                        fill(b0, b1, c)
                        if b1 is not None:
                            rank(b1, c, banks)
                    if b1 is not None:
                        pe.wait_ge(x_low, b1 + 1 + CREDIT)
                        spread_x(b1, 0)
                        for g in range(2):
                            mod_ffn(b1, g)

                def slot(b0, b1, k):
                    if b1 is not None and k > 0:
                        spread_x(b1, k)
                    if b0 is not None:
                        if k < 4:
                            hidden(b0, "h2", 0, k)
                        elif k == 4:
                            ffn_out(b0, 0)
                            value(b0, 0)
                            ffn_in(b0, 1, 0)
                        elif k == 5:
                            ffn_in(b0, 1, 1)
                            ffn_in(b0, 1, 2)
                        elif k == 6:
                            ffn_in(b0, 1, 3)
                        elif 7 <= k < 11:
                            hidden(b0, "h1", 1, k - 7)
                        elif 11 <= k < 15:
                            hidden(b0, "h2", 1, k - 11)
                        else:
                            ffn_out(b0, 1)
                            value(b0, 1)
                    if b1 is not None and k > 0:
                        gather_y(b1, k - 1)

                def finish(b1):
                    gather_y(b1, NGRP - 1)
                    for g in range(2):
                        bank = open1d(b1, ("out", g))
                        pe.wait_ge(yg_ready, b1 * 2 + (g + 1) + CREDIT)
                        pe.matmul(bank[:], W_OUT, yg[:, hs_(g)], start=True, stop=True).then_inc(l1_dve_full, 1)

                def stage(b0, b1, first=False):
                    before_states(b0, b1, first)
                    for k in range(NGRP):
                        slot(b0, b1, k)
                    if b1 is not None:
                        finish(b1)

                stage(0, None, first=True)
                pe.wait_ge(l1_params, 16 * NPARAM_L1)
                with pe.Fori(0, BATCH - 1) as b:
                    stage(b + 1, b)
                stage(None, BATCH - 1)

            for semaphore in (l0_act_full, l0_dve_full, l1_act_full, l1_dve_full, y_full, ranked):
                pe.sem_inc(semaphore, CREDIT)
            pe.wait_ge(wk_ready, 1)
            pe.matmul(bank0d[:, 0:P], rw[:, 0, :], wk_th[:], start=True, stop=True).then_inc(qk_full, 1)
            pe.wait_ge(qk_ready, 1)
            retention_in(0)
            retention_chunks(0)
            pe.wait_ge(consts_set, 4)
            pe.wait_ge(inexact_ready, 1)
            pe.matmul(bank1a[:, 0:len(FFN_WEIGHTS)], ones[:], inexact_b[:], start=True, stop=True).then_inc(inexact_full, 1)
            pe.wait_ge(inexact_known, 1)
            has_low = pe.value_load(inexact_i[0:1, 0:1], min_val=0, max_val=P * len(FFN_WEIGHTS))
            with pe.If(has_low):
                rest(exact=False)
            with pe.Else():
                rest(exact=True)

        @block.vector
        def _(dve):
            for semaphore in (stats0, aggr0, xn_ready, xg_ready, l0_dve_done, mem_step, x1_ready, stats1, aggr1,
                              l1_dve_done, tie_ready, beats_ready, sigh_ready, conv_step, mod_ready, u_ready,
                              yd_ready, yg_ready, o_ready, x_low, pad_ready):
                dve.sem_inc(semaphore, CREDIT)

            def full0(b, job):
                dve.wait_ge(l0_dve_full, after(b, L0_DVE, job))

            def full1(b, job):
                dve.wait_ge(l1_dve_full, after(b, L1_DVE, job))
                return bank1d[L1_DVE.index(job) % 2]

            def norm_l0(b):
                dve.wait_ge(x_tok_in, b * 16 + 16)
                for c in range(CH):
                    last = dve.bn_stats(st0[:, c, :], xt[:, c, :])
                last.then_inc(stats0, 1)
                dve.wait_ge(stats0, b + 1 + CREDIT)
                dve.memset(wait_carrier[:], 0.0)
                for c in range(CH):
                    last = dve.bn_aggr(mv0[:, c, :], st0[:, c, :])
                last.then_inc(aggr0, 1)
                dve.wait_ge(aggr0, b + 1 + CREDIT)
                dve.wait_ge(rstd0_ready, b + 1 + CREDIT)
                for g in range(2):
                    for c in range(g * CPH, (g + 1) * CPH):
                        last = dve.tensor_scalar(xn[:, c, :], xt[:, c, :], mv0[:, c, 0:1], rstd0[:, c:c + 1],
                                                 ALU.subtract, ALU.mult)
                    last.then_inc(xn_ready, 1)
                dve.wait_ge(xn_ready, b * 2 + 2 + CREDIT)
                if isinstance(b, int) and b == 0:
                    dve.wait_ge(params, 16 * NPARAM)
                dve.tensor_scalar(xg[:], xn[:], scale("gamma_col"), None, ALU.mult).then_inc(xg_ready, 1)

            def chunks(b):
                for g in range(2):
                    cs = slice(g * CPH, (g + 1) * CPH)
                    full0(b, ("scores", g))
                    dve.tensor_tensor(sc[:, cs, :], bank0d[:].rearrange("p (c i) -> p c i", i=P),
                                      mask[:].rearrange("p (o i) -> p o i", o=1).broadcast_to([P, CPH, P]),
                                      ALU.mult).then_inc(l0_dve_done, 1)
                    full0(b, ("outer", g))
                    for c in range(g * CPH, (g + 1) * CPH):
                        if c == CPH:
                            dve.wait_ge(l0_dve_done, after(b, L0_DVE, ("outer", 0)))
                        elif c > 0:
                            dve.wait_ge(mem_step, b * MEM_STEPS + (c - g) + CREDIT)
                        last = dve.scalar_tensor_tensor(mem[:, c + 1, :], mem[:, c, :], GAMMA ** P,
                                                        bank0d[:, ck(c - g * CPH)], ALU.mult, ALU.add)
                        if c + 1 in ((g + 1) * CPH, CH - 1):
                            last.then_inc(l0_dve_done, 1)
                            break
                        last.then_inc(mem_step, 1)

            def z_product(b, g, m):
                k = HIDDEN.index(("z", g, m))
                full0(b, ("z2", g, m))
                dve.wait_ge(l0_act_done, after(b, L0_ACT, ("z1", g, m)))
                dve.wait_ge(hidden_low, b * len(HIDDEN) + (max(k - NPLAIN + 1, 0) + CREDIT))
                dve.scalar_tensor_tensor(plain[:, k % NPLAIN, :], bank0d[:], scale("w2_s", m), silu1[:, m % 2, :],
                                         ALU.mult, ALU.mult).then_inc(l0_dve_done, 1)

            def residual_l0(b, g):
                full0(b, ("s", g))
                dve.wait_ge(l0_act_done, after(b, L0_ACT, ("w3", g)))
                dve.wait_ge(res_ready, b + CREDIT)
                dve.tensor_tensor(sg[:, hs_(g)], bank0d[:], g0[:, hs_(g)], ALU.mult).then_inc(l0_dve_done, 1)
                dve.wait_ge(l0_dve_done, after(b, L0_DVE, ("s", g)))
                dve.wait_ge(x_feat_in, b * 16 + 16)
                dve.tensor_tensor(x1[:, hs_(g)], sg[:, hs_(g)], xf[:, hs_(g)], ALU.add).then_inc(x1_ready, 1)

            def norm_l1(b):
                dve.wait_ge(p_ready, b * NGRP + CREDIT)
                dve.memset(ssm[:, 0:TAPS - 1], 0.0).then_inc(pad_ready, 1)
                for g in range(2):
                    bank = full1(b, ("tok", g))
                    for c in range(g * CPH, (g + 1) * CPH):
                        last = dve.bn_stats(st1[:, c, :], bank[:, ck(c - g * CPH)])
                    last.then_inc(stats1, 1)
                    dve.wait_ge(stats1, b * 2 + (g + 1) + CREDIT)
                    dve.memset(wait_carrier[:], 0.0)
                    for c in range(g * CPH, (g + 1) * CPH):
                        last = dve.bn_aggr(mv1[:, c, :], st1[:, c, :])
                    last.then_inc(aggr1, 1)
                for g in range(2):
                    bank = bank1d[L1_DVE.index(("tok", g)) % 2]
                    dve.wait_ge(rstd1_ready, b * 2 + (g + 1) + CREDIT)
                    dve.wait_ge(aggr1, b * 2 + (g + 1) + CREDIT)
                    for c in range(g * CPH, (g + 1) * CPH):
                        last = dve.tensor_scalar(yn[:, c, :], bank[:, ck(c - g * CPH)], mv1[:, c, 0:1],
                                                 rstd1[:, c:c + 1], ALU.subtract, ALU.mult)
                    last.then_inc(l1_dve_done, 1)

            def score_columns(b):
                for g in range(2):
                    bank = full1(b, ("score_col", g))
                    dve.tensor_copy(scol[:, g * CPH:(g + 1) * CPH],
                                    bank[:].rearrange("p (c i) -> p c i", i=P)[:, :, 0]).then_inc(l1_dve_done, 1)

            def convolution(b):
                dve.wait_ge(l1_act_done, after(b, L1_ACT, ("ssm", 1)))
                dve.wait_ge(pad_ready, b + 1 + CREDIT)
                dve.tensor_scalar(cv[0][:], ssm[:, 0:SEQ], scale("conv_w", 0), None, ALU.mult).then_inc(conv_step, 1)
                for k in range(1, TAPS):
                    dve.wait_ge(conv_step, b * TAPS + k + CREDIT)
                    dve.scalar_tensor_tensor(cv[k % 2][:], ssm[:, k:k + SEQ], scale("conv_w", k), cv[(k + 1) % 2][:],
                                             ALU.mult, ALU.add).then_inc(conv_step, 1)

            def low_x(b):
                dve.wait_ge(x_high, b + 1 + CREDIT)
                for half in range(2):
                    rows = slice(half * P // 2, (half + 1) * P // 2)
                    other = slice((1 - half) * P // 2, (2 - half) * P // 2)
                    last = dve.tensor_tensor(xpair[other, half, :], xc[rows, :], xpair[rows, half, :].bitcast(F32),
                                             ALU.subtract)
                last.then_inc(x_low, 1)

            def compare(b):
                dve.wait_ge(l1_dve_done, after(b, L1_DVE, ("score_col", 1)))
                for c in range(CH):
                    dve.scalar_tensor_tensor(tie[:, c, :], srow[:, ck(c)], scol[:, c:c + 1], tri[:],
                                             ALU.is_equal, ALU.mult).then_inc(tie_ready, 1)
                for c in range(CH):
                    if c >= 2:
                        dve.wait_ge(ranked, b * (CH - 1) + (c - 1) + CREDIT)
                    s_i = scol[:, c:c + 1]
                    bt = beats[:, c % 2, :]
                    if c > 0:
                        dve.tensor_scalar(bt[:, 0:c * P], srow[:, 0:c * P], s_i, None, ALU.is_lt)
                    if c < CH - 1:
                        dve.tensor_scalar(bt[:, (c + 1) * P:], srow[:, (c + 1) * P:], s_i, None, ALU.is_le)
                    dve.wait_ge(tie_ready, b * CH + (c + 1) + CREDIT)
                    dve.scalar_tensor_tensor(bt[:, ck(c)], srow[:, ck(c)], s_i, tie[:, c, :],
                                             ALU.is_lt, ALU.add).then_inc(beats_ready, 1)

            def token_weights(b):
                dve.wait_ge(sig_ready, b + 1 + CREDIT)
                dve.tensor_scalar(g1[:], g1[:], 0.5, 0.5, ALU.mult, ALU.add).then_inc(sigh_ready, 1)
                dve.wait_ge(sigh_ready, b + 1 + CREDIT)
                for g in range(2):
                    bank = full1(b, ("rank", g))
                    dve.scalar_tensor_tensor(g1[:, hs_(g)], bank[:], float(TOPK), g1[:, hs_(g)],
                                             ALU.is_lt, ALU.mult).then_inc(l1_dve_done, 1)

            def mod_update(b):
                for g in range(2):
                    bank = full1(b, ("ffn", g))
                    dve.wait_ge(l1_dve_done, after(b, L1_DVE, ("rank", g)))
                    dve.scalar_tensor_tensor(g1[:, hs_(g)], bank[:], scale("b2"), g1[:, hs_(g)],
                                             ALU.add, ALU.mult).then_inc(l1_dve_done, 1)
                for g in range(2):
                    dve.wait_ge(l1_dve_done, after(b, L1_DVE, ("ffn", g)))
                    dve.tensor_tensor(g1[:, hs_(g)], g1[:, hs_(g)], ynT[:, hs_(g)], ALU.add).then_inc(mod_ready, 1)

            def states(b, gr):
                if gr == 0:
                    dve.wait_ge(l1_act_done, after(b, L1_ACT, ("B", 1)))
                for g in range(2):
                    bank = full1(b, ("xs", gr, g))
                    dve.tensor_tensor(bank[:], bank[:], Bt[:, hs_(g)], ALU.mult).then_inc(u_ready, 1)
                dve.wait_ge(p_ready, b * NGRP + (max(gr - 1, 0) + CREDIT))
                for g in range(2):
                    bank = bank1d[L1_DVE.index(("xs", gr, g)) % 2]
                    dve.wait_ge(u_ready, b * 2 * NGRP + (2 * gr + g + 1) + CREDIT)
                    h = hs[:, gr % 2, :]
                    if g == 1:
                        dve.wait_ge(l1_dve_done, after(b, L1_DVE, ("xs", gr, 0)))
                    dve.tensor_tensor_scan(h[:, hs_(g)], decay[:, gr:gr + 1].broadcast_to([P, HALF]), bank[:],
                                           0.0 if g == 0 else h[:, HALF - 1:HALF],
                                           ALU.mult, ALU.add).then_inc(l1_dve_done, 1)

            def finish(b):
                dve.wait_ge(y_full, b * NGRP + NGRP + CREDIT)
                for g in range(2):
                    dve.scalar_tensor_tensor(yg[:, hs_(g)], xc[:, hs_(g)], scale("D"), ybank[g][:],
                                             ALU.mult, ALU.add).then_inc(yd_ready, 1)
                for g in range(2):
                    dve.wait_ge(yd_ready, b * 2 + (g + 1) + CREDIT)
                    dve.tensor_tensor(yg[:, hs_(g)], yg[:, hs_(g)], gate[:, hs_(g)], ALU.mult).then_inc(yg_ready, 1)
                for g in range(2):
                    bank = full1(b, ("out", g))
                    dve.wait_ge(g1_ready, b * 2 + (g + 1) + CREDIT)
                    dve.scalar_tensor_tensor(o[:, hs_(g)], bank[:], scale("b_out"), g1[:, hs_(g)],
                                             ALU.add, ALU.mult).then_inc(l1_dve_done, 1)
                for g in range(2):
                    dve.wait_ge(l1_dve_done, after(b, L1_DVE, ("out", g)))
                    dve.wait_ge(res_ready, b + 1 + CREDIT)
                    dve.tensor_tensor(o[:, hs_(g)], o[:, hs_(g)], res[:, hs_(g)], ALU.add).then_inc(o_ready, 1)

            def before_states(b0, b1):
                if b0 is not None and b1 is not None:
                    norm_l0(b0)
                if b1 is not None:
                    norm_l1(b1)
                if b0 is not None:
                    if b1 is not None:
                        chunks(b0)
                    for m in range(KT):
                        z_product(b0, 0, m)
                if b1 is not None:
                    score_columns(b1)
                    convolution(b1)
                    compare(b1)
                    low_x(b1)
                    token_weights(b1)

            def slot(b0, b1, k):
                if b1 is not None:
                    states(b1, k)
                    if k == 0:
                        mod_update(b1)
                if b0 is not None:
                    if k == 4:
                        residual_l0(b0, 0)
                        z_product(b0, 1, 0)
                    elif k == 5:
                        z_product(b0, 1, 1)
                        z_product(b0, 1, 2)
                    elif k == 6:
                        z_product(b0, 1, 3)
                    elif k == 15:
                        residual_l0(b0, 1)

            def stage(b0, b1):
                before_states(b0, b1)
                for k in range(NGRP):
                    slot(b0, b1, k)
                if b1 is not None:
                    finish(b1)

            dve.wait_ge(params, 16 * NPARAM)
            dve.wait_ge(theta_ready, 1)
            dve.tensor_scalar(wk_th[:], rw[:, 1, :], theta1[:, 0:1], theta1[:, 0:1], ALU.mult, ALU.mult).then_inc(wk_ready, 1)
            dve.wait_ge(consts_set, 4)
            norm_l0(0)
            dve.wait_ge(qk_full, 1)
            dve.tensor_copy(qk[:], bank0d[:, 0:P]).then_inc(qk_ready, 1)
            chunks(0)
            for i, (raw, high, low) in enumerate(FFN_WEIGHTS):
                dve.wait_ge(weight_high, i + 1)
                dve.tensor_tensor(low, raw, high.bitcast(F32), ALU.subtract).then_inc(weight_low, 1)
                dve.wait_ge(weight_low, i + 1)
                dve.tensor_reduce(inexact[:, i:i + 1], low.bitcast(F32), mybir.AxisListType.X, ALU.max,
                                  apply_absolute_value=True).then_inc(inexact_step, 1)
            dve.wait_ge(inexact_step, len(FFN_WEIGHTS))
            dve.tensor_scalar(inexact_b[:], inexact[:], 0.0, None, ALU.not_equal).then_inc(inexact_ready, 1)
            dve.wait_ge(inexact_full, 1)
            dve.tensor_reduce(inexact[:, 0:1], bank1a[:, 0:len(FFN_WEIGHTS)], mybir.AxisListType.X, ALU.add).then_inc(inexact_step, 1)
            dve.wait_ge(inexact_step, len(FFN_WEIGHTS) + 1)
            dve.tensor_copy(inexact_i[:], inexact[:, 0:1]).then_inc(inexact_known, 1)
            stage(0, None)
            dve.wait_ge(l1_params, 16 * NPARAM_L1)
            dve.wait_ge(decay_ready, 1)
            with dve.Fori(0, BATCH - 1) as b:
                stage(b + 1, b)
            stage(None, BATCH - 1)


def constants():
    i = np.arange(P)
    diff = i[None, :] - i[:, None]
    decay_mask = np.where(diff >= 0, GAMMA ** np.maximum(diff, 0), 0.0)
    gamma_row = np.broadcast_to(GAMMA ** (i + 1.0), (P, P))
    before_mask = (i[:, None] < i[None, :]).astype(np.float32)
    n, dd = i // DPG, i % DPG
    spread = np.zeros((P, NGRP // 2, P), np.float32)
    for g in range(NGRP // 2):
        for part in range(2):
            spread[part * P // 2 + DPG * g + dd, g, i] = 1.0
    gather = np.zeros((P, 2 * P - DPG), np.float32)
    gather[i, P - DPG + dd] = 1.0
    return {"decay_mask": decay_mask.astype(np.float32), "gamma_row": gamma_row.astype(np.float32),
            "identity": np.eye(P, dtype=np.float32), "before_mask": before_mask,
            "spread": spread.reshape(P, -1), "gather": gather,
            "gamma_col": (GAMMA ** (P - 1.0 - i)).astype(np.float32)[:, None]}


def kernel(**inputs):
    import concourse.bacc as bacc
    from concourse.bass_utils import run_bass_kernel_spmd

    a = {k: np.asarray(v) for k, v in inputs.items()}
    c = constants()
    x = a["L0_attn_x"]

    def columns(v):
        return v.reshape(-1, P).T

    def k_tiles(w):
        return w.reshape(-1, P, w.shape[1]).transpose(1, 0, 2)

    a_log = a["L1_attn_A_log"].reshape(NGRP, DPG, NSTATE).transpose(2, 1, 0).reshape(P, NGRP)
    w_x, b_x = a["L1_attn_W_x"], a["L1_attn_b_x"]
    cols = {"w1_s": columns(a["L0_ffn_w1_s"]), "w2_s": columns(a["L0_ffn_w2_s"]), "h1_s": columns(a["L0_ffn_h1_s"]),
            "h2_s": columns(a["L0_ffn_h2_s"]), "w3_s": columns(a["L0_ffn_w3_s"]), "theta": columns(a["L0_attn_theta"]),
            "b_in": columns(a["L1_attn_b_in"]), "conv_w": a["L1_attn_conv_w"], "conv_b": columns(a["L1_attn_conv_b"]),
            "D": columns(a["L1_attn_D_param"]), "b_out": columns(a["L1_attn_b_out"]), "b1": columns(a["L1_ffn_b1"]),
            "b2": columns(a["L1_ffn_b2"]), "b_x": np.repeat(b_x, DPG).reshape(2, P).T, "A_log": a_log,
            "gamma_col": c.pop("gamma_col")}
    arrays = {
        "x_tok": x.reshape(BATCH, CH, P, P).transpose(0, 2, 1, 3),
        "x_feat": x.transpose(0, 2, 1),
        "small": np.concatenate([cols[k] for k in COLS], axis=1),
        "w_in0": np.concatenate([a["L0_ffn_w1_w"].T, a["L0_ffn_w2_w"].T], axis=1),
        "h_w": np.stack([k_tiles(a["L0_ffn_h1_w"].T), k_tiles(a["L0_ffn_h2_w"].T)], axis=1).reshape(P, 2, -1),
        "w3T": k_tiles(a["L0_ffn_w3_w"].T).reshape(P, -1),
        "retention_w": np.stack([a["L0_attn_weight_q"].T, a["L0_attn_weight_k"].T, a["L0_attn_weight_v"]], axis=1),
        "l1_w": np.concatenate([a["L1_attn_W_in"], np.repeat(w_x, DPG, axis=1),
                                np.repeat(a["L1_ffn_w_router"][:, None], P, axis=1), a["L1_attn_W_out"],
                                a["L1_ffn_W1"]], axis=1),
        "w2_l1": k_tiles(a["L1_ffn_W2"]),
        **c,
    }
    nc = bacc.Bacc("TRN2", target_bir_lowering=False, num_devices=1)
    aps = {}
    for name, value in arrays.items():
        arrays[name] = np.ascontiguousarray(value)
        aps[name] = nc.dram_tensor(name, arrays[name].shape, mybir.dt.from_np(arrays[name].dtype),
                                   kind="ExternalInput").ap()
    out = nc.dram_tensor("out", (BATCH, P, SEQ), F32, kind="ExternalOutput").ap()
    program(nc, out=out, **aps)
    got = run_bass_kernel_spmd(nc, [arrays], core_ids=[0]).results[0]["out"]
    return np.ascontiguousarray(got.transpose(0, 2, 1))
```

```python
from contextlib import ExitStack

import numpy as np

import concourse.bass as bass
from concourse import mybir

F32 = mybir.dt.float32
F32R = mybir.dt.float32r
BF16 = mybir.dt.bfloat16
I32 = mybir.dt.int32
ALU = mybir.AluOpType
ACT = mybir.ActivationFunctionType

P = 128
BATCH = 4
SEQ = 1024
HALF = 512
CH = SEQ // P
CPH = HALF // P
HID = 512
KT = HID // P
NSTATE = 16
DPG = P // NSTATE
NGRP = P // DPG
TAPS = 4
CREDIT = 1
MEM_STEPS = CH - 3
TOPK = SEQ // 2
GAMMA = 0.96875
EPS = 1e-5

MOD_UP, MOD_DOWN = (2, 9), (6, 13)
L0_OUT = (5, 12)
TO_TOKENS = 14
STATS_L0, RSTD_L0, NORM_L0 = 7, 8, 9

COLS = {}
_at = 0
for _name, _n in [("w1_s", KT), ("w2_s", KT), ("h1_s", KT), ("h2_s", KT), ("w3_s", 1), ("theta", 1),
                  ("b_in", 2), ("conv_w", TAPS), ("conv_b", 1), ("D", 1), ("b_out", 1), ("b1", KT),
                  ("b2", 1), ("b_x", 2), ("A_log", NGRP), ("gamma_col", 1)]:
    COLS[_name] = slice(_at, _at + _n)
    _at += _n
NCOLS = _at

L0_ACT = ([("xnT", g) for g in range(2)] + [("q", g) for g in range(2)]
          + [("z1", 0, 0), ("z1", 0, 1), ("z1", 0, 2), ("u", 0), ("z1", 0, 3), ("u", 1)]
          + [("h1", 0, m) for m in range(KT)] + [("h2", 0, m) for m in range(KT)]
          + [("z1", 1, m) for m in range(KT)] + [("w3", 0)]
          + [("h1", 1, m) for m in range(KT)] + [("h2", 1, m) for m in range(KT)] + [("w3", 1)]
          + [("tok", g) for g in range(2)])
L0_DVE = ([(k, g) for g in range(2) for k in ("scores", "outer")]
          + [("z2", g, m) for g in range(2) for m in range(KT)] + [("s", g) for g in range(2)])
L1_ACT = ([(k, g) for k in ("xnT", "ssm", "score", "gate", "B", "C") for g in range(2)]
          + [("ffn", g, m) for g in range(2) for m in range(KT)])
L1_DVE = [(k, g) for k in ("score_col", "rank") for g in range(2)]
for _gr in range(NGRP):
    L1_DVE += [("xs", _gr, g) for g in range(2)]
    if _gr in MOD_DOWN:
        L1_DVE.append(("ffn", MOD_DOWN.index(_gr)))
L1_DVE += [("out", g) for g in range(2)]
HIDDEN = [(k, g, m) for g, k in ((0, "z"), (0, "h1"), (0, "h2"), (1, "z"), (1, "h1"), (1, "h2")) for m in range(KT)]
HIDDEN_IN_SLOT = [[] for _ in range(NGRP)]
for _k, _g, _slot in (("h2", 0, 0), ("z", 1, 3), ("h1", 1, 7), ("h2", 1, 10)):
    for _m in range(KT):
        HIDDEN_IN_SLOT[_slot + _m // 2].append((_k, _g, _m))
NPLAIN = 3


def mod_up_in_slot(k, alone):
    if alone:
        return [(g, k - at) for g, at in ((0, 0), (1, MOD_DOWN[0] + 1)) if 0 <= k - at < KT]
    return [(MOD_UP.index(k), m) for m in range(KT)] if k in MOD_UP else []


def after(b, order, job):
    return b * len(order) + (order.index(job) + 1 + CREDIT)


def program(nc, x_tok, x_feat, small, w_in0, h_w, w3T, retention_w, l1_w, w2_l1, decay_mask, gamma_row,
            identity, before_mask, spread, gather, out):
    with ExitStack() as ctx:
        def sb(name, shape, dt=F32):
            return ctx.enter_context(nc.sbuf_tensor(name, shape, dt))

        def ps(name, shape, dt=F32):
            return ctx.enter_context(nc.psum_tensor(name, shape, dt))

        def sem(name):
            return ctx.enter_context(nc.semaphore(name))

        col = sb("col", [P, NCOLS])
        w12h = sb("w12h", [P, 2, HID], F32R)
        w12l = sb("w12l", [P, 2, HID], F32R)
        hTh = sb("hTh", [P, 2, KT, HID], F32R)
        hTl = sb("hTl", [P, 2, KT, HID], F32R)
        w3h = sb("w3h", [P, KT, P], F32R)
        w3l = sb("w3l", [P, KT, P], F32R)
        rw = sb("rw", [P, 3, P])
        lw = sb("lw", [P, 6 * P + HID])
        w2l = sb("w2l", [P, KT, P])
        mask = sb("mask", [P, P])
        grow = sb("grow", [P, P])
        ident = sb("ident", [P, P])
        tri = sb("tri", [P, P])
        spr = sb("spr", [P, NGRP // 2, P], F32R)
        gat = sb("gat", [P, 2 * P - DPG])
        ones = sb("ones", [P, P], BF16)
        half_neg = sb("half_neg", [P, CH])
        eps = sb("eps", [P, CH])
        wait_carrier = sb("wait_carrier", [P, 3])
        theta1 = sb("theta1", [P, 1])
        wk_th = sb("wk_th", [P, P])
        qk = sb("qk", [P, P])
        aexp = sb("aexp", [P, NGRP])
        decay = sb("decay", [P, NGRP])
        inexact = sb("inexact", [P, 4])
        inexact_b = sb("inexact_b", [P, 4], BF16)
        inexact_i = sb("inexact_i", [P, 1], I32)
        W_IN, W_B, W_C, W_R, W_OUT, W_1 = (lw[:, 0:2 * P], lw[:, 2 * P:3 * P], lw[:, 3 * P:4 * P],
                                           lw[:, 4 * P:5 * P], lw[:, 5 * P:6 * P], lw[:, 6 * P:])

        xt = sb("xt", [P, CH, P])
        xg = xt
        xf = sb("xf", [P, SEQ])
        st0 = sb("st0", [P, CH, 6])
        mv0 = sb("mv0", [P, CH, 2])
        ve0 = sb("ve0", [P, CH])
        rstd0 = sb("rstd0", [P, CH])
        xn = sb("xn", [P, CH, P])
        xnT = sb("xnT", [P, SEQ])
        xnTh = sb("xnTh", [P, SEQ], F32R)
        xnTl = sb("xnTl", [P, SEQ], F32R)
        q = sb("q", [P, SEQ])
        qg = q
        u = q
        sc = sb("sc", [P, CH, P])
        g0 = sc[:].rearrange("p c i -> p (c i)")
        mem = sb("mem", [P, CH + 1, P])
        plain = sb("plain", [P, NPLAIN, HALF])
        hidAh = sb("hidAh", [P, KT, HALF], F32R)
        hidAl = sb("hidAl", [P, KT, HALF], F32R)
        hidBh = sb("hidBh", [P, KT, HALF], F32R)
        hidBl = sb("hidBl", [P, KT, HALF], F32R)
        A, B = (hidAh, hidAl), (hidBh, hidBl)
        pair = {("z", 0): A, ("h1", 0): B, ("h2", 0): A, ("z", 1): B, ("h1", 1): A, ("h2", 1): B}
        x1 = sb("x1", [P, SEQ])
        sg = x1

        res = sb("res", [P, SEQ])
        st1 = sb("st1", [P, CH, 6])
        mv1 = sb("mv1", [P, CH, 2])
        ve1 = sb("ve1", [P, CH])
        rstd1 = sb("rstd1", [P, CH])
        early = sb("early", [P, 2 * SEQ])
        yn = early[:, 0:SEQ].rearrange("p (c d) -> p c d", d=P)
        tie = yn
        beats = early[:, SEQ:2 * SEQ].bitcast(BF16).rearrange("p (a t) -> p a t", a=2)
        fh = early[:].rearrange("p (k t) -> p k t", k=KT)
        ynT = sb("ynT", [P, SEQ])
        srow = sb("srow", [P, SEQ])
        scol = sb("scol", [P, CH])
        hs = sb("hs", [P, 2, SEQ])
        ssm = hs[:].rearrange("p a t -> p (a t)")[:, 0:TAPS - 1 + SEQ]
        xc = sb("xc", [P, SEQ])
        xpair = sb("xpair", [P, 2, SEQ], F32R)
        Bt = sb("Bt", [P, SEQ])
        yg = Bt
        cv = [Bt, xc]
        Ct = sb("Ct", [P, SEQ])
        gate = mem[:, 1:CH + 1, :].rearrange("p c i -> p (c i)")
        g1 = sb("g1", [P, SEQ])
        pr = sb("pr", [P, 2, SEQ])

        bank0a = [ps(f"bank0a{i}", [P, HALF]) for i in range(2)]
        bank0d = ps("bank0d", [P, HALF])
        bank1a = ps("bank1a", [P, HALF])
        bank1d = [ps(f"bank1d{i}", [P, HALF]) for i in range(2)]
        ybank = [ps(f"ybank{i}", [P, HALF]) for i in range(2)]

        l0_dve_full = sem("l0_dve_full")
        x_tok_in = sem("x_tok_in")
        x1_ready = sem("x1_ready")
        x_feat_in = sem("x_feat_in")
        o_ready = sem("o_ready")
        stored = sem("stored")
        params = sem("params")
        consts_set = sem("consts_set")
        aggr0 = sem("aggr0")
        eps0 = sem("eps0")
        rstd0_ready = sem("rstd0_ready")
        aggr1 = sem("aggr1")
        eps1 = sem("eps1")
        rstd1_ready = sem("rstd1_ready")
        l0_act_done = sem("l0_act_done")
        xn_low = sem("xn_low")
        qg_ready = sem("qg_ready")
        z_high = sem("z_high")
        hidden_low = sem("hidden_low")
        l1_act_done = sem("l1_act_done")
        y_full = sem("y_full")
        l1_dve_done = sem("l1_dve_done")
        p_ready = sem("p_ready")
        pad_ready = sem("pad_ready")
        l1_params = sem("l1_params")
        yn_ready = sem("yn_ready")
        p_half = sem("p_half")
        y_half = sem("y_half")
        weight_low_h = sem("weight_low_h")
        states_ready = sem("states_ready")
        theta_ready = sem("theta_ready")
        aexp_ready = sem("aexp_ready")
        decay_ready = sem("decay_ready")
        weight_high = sem("weight_high")
        l0_act_full = sem("l0_act_full")
        l1_act_full = sem("l1_act_full")
        l0_dve_done = sem("l0_dve_done")
        res_ready = sem("res_ready")
        mod_ready = sem("mod_ready")
        yg_ready = sem("yg_ready")
        conv_step = sem("conv_step")
        xc_ready = sem("xc_ready")
        x_high = sem("x_high")
        sig_ready = sem("sig_ready")
        l1_dve_full = sem("l1_dve_full")
        g1_ready = sem("g1_ready")
        spr_ready = sem("spr_ready")
        weight_low = sem("weight_low")
        xn_ready = sem("xn_ready")
        xg_ready = sem("xg_ready")
        beats_ready = sem("beats_ready")
        ranked = sem("ranked")
        yd_ready = sem("yd_ready")
        x_low = sem("x_low")
        wk_ready = sem("wk_ready")
        qk_full = sem("qk_full")
        qk_ready = sem("qk_ready")
        inexact_ready = sem("inexact_ready")
        inexact_full = sem("inexact_full")
        inexact_known = sem("inexact_known")
        stats0 = sem("stats0")
        mem_step = sem("mem_step")
        stats1 = sem("stats1")
        tie_ready = sem("tie_ready")
        sigh_ready = sem("sigh_ready")
        inexact_step = sem("inexact_step")
        raw_loaded = [sem(f"raw_loaded{i}") for i in range(4)]
        NPARAM = 5
        NPARAM_L1 = 5

        hs_ = lambda g: slice(g * HALF, (g + 1) * HALF)
        ck = lambda c: slice(c * P, (c + 1) * P)

        def scale(name, m=0):
            s = COLS[name].start + m
            return col[:, s:s + 1]

        raw_h = [hs[:].rearrange("p a t -> p (a t)"), pr[:].rearrange("p a t -> p (a t)")]
        raw_w12, raw_w3 = Bt[:], Ct[:, 0:KT * P]
        raw_spr = g1[:, 0:NGRP // 2 * P]
        FFN_WEIGHTS = [(raw_w12, w12h[:].rearrange("p a n -> p (a n)"), w12l[:].rearrange("p a n -> p (a n)"))]
        for i in range(2):
            FFN_WEIGHTS.append((raw_h[i], hTh[:, i].rearrange("p k n -> p (k n)"),
                                hTl[:, i].rearrange("p k n -> p (k n)")))
        FFN_WEIGHTS.append((raw_w3, w3h[:].rearrange("p k n -> p (k n)"), w3l[:].rearrange("p k n -> p (k n)")))

        block = ctx.enter_context(nc.Block())

        @block.sync
        def _(sp):
            def load_x(b):
                sp.wait_ge(l0_dve_full, (b - 1) * len(L0_DVE) + (L0_DVE.index(("outer", 1)) + 1 + CREDIT))
                sp.dma_start(xt[:], x_tok[bass.ds(b, 1)].rearrange("o p c d -> (o p) c d")).then_inc(x_tok_in, 16)
                sp.wait_ge(x1_ready, b * 2 + CREDIT)
                sp.dma_start(xf[:], x_feat[bass.ds(b, 1)].rearrange("o p t -> (o p) t")).then_inc(x_feat_in, 16)

            def store(b):
                for g in range(2):
                    sp.wait_ge(o_ready, b * 2 + (g + 1) + CREDIT)
                    sp.dma_start(out[bass.ds(b, 1), :, hs_(g)].rearrange("o p t -> (o p) t"), res[:, hs_(g)]).then_inc(stored, 16)

            sp.dma_start(xt[:], x_tok[0]).then_inc(x_tok_in, 16)
            sp.dma_start(ident[:], identity).then_inc(params, 16)
            sp.dma_start(col[:], small).then_inc(params, 16)
            sp.dma_start(rw[:], retention_w).then_inc(params, 16)
            sp.dma_start(raw_w12, w_in0).then_inc(raw_loaded[0], 16)
            for i in range(2):
                sp.dma_start(raw_h[i], h_w[:, i]).then_inc(raw_loaded[1 + i], 16)
            sp.dma_start(raw_w3, w3T).then_inc(raw_loaded[3], 16)
            sp.dma_start(xf[:], x_feat[0]).then_inc(x_feat_in, 16)
            sp.sem_inc(stored, CREDIT)
            load_x(1)
            with sp.Fori(0, BATCH - 2) as b:
                load_x(b + 2)
                store(b)
            store(BATCH - 2)
            store(BATCH - 1)
            sp.wait_ge(stored, BATCH * 2 * 16 + CREDIT)

        @block.gpsimd
        def _(pool):
            pool.memset(eps[:], EPS).then_inc(consts_set, 1)
            pool.memset(half_neg[:], -0.5).then_inc(consts_set, 1)
            pool.memset(mem[:, 0, :], 0.0).then_inc(consts_set, 1)
            pool.memset(ones[:], 1.0).then_inc(consts_set, 1)

            def rstd_l0(b):
                pool.wait_ge(aggr0, b + 1 + CREDIT)
                pool.tensor_tensor(ve0[:], mv0[:, :, 1], eps[:], ALU.add).then_inc(eps0, 1)
                pool.wait_ge(eps0, b + 1 + CREDIT)
                pool.tensor_tensor(rstd0[:], ve0[:], half_neg[:], ALU.pow).then_inc(rstd0_ready, 1)

            def rstd_l1(b):
                for g in range(2):
                    c = slice(g * CPH, (g + 1) * CPH)
                    pool.wait_ge(aggr1, b * 2 + (g + 1) + CREDIT)
                    pool.tensor_tensor(ve1[:, c], mv1[:, c, 1], eps[:, c], ALU.add).then_inc(eps1, 1)
                    pool.wait_ge(eps1, b * 2 + (g + 1) + CREDIT)
                    pool.tensor_tensor(rstd1[:, c], ve1[:, c], half_neg[:, c], ALU.pow).then_inc(rstd1_ready, 1)

            def low_xn(b, g):
                pool.wait_ge(l0_act_done, after(b, L0_ACT, ("xnT", g)))
                pool.tensor_tensor(xnTl[:, hs_(g)], xnT[:, hs_(g)], xnTh[:, hs_(g)].bitcast(F32),
                                   ALU.subtract).then_inc(xn_low, 1)

            def scale_q(b, g):
                pool.wait_ge(l0_dve_full, after(b, L0_DVE, ("scores", g)))
                v = lambda t: t[:, hs_(g)].rearrange("p (c i) -> p c i", i=P)
                pool.tensor_tensor(v(qg), v(q), grow[:].rearrange("p (o i) -> p o i", o=1).broadcast_to([P, CPH, P]),
                                   ALU.mult).then_inc(qg_ready, 1)

            def low_hidden(b, kind, g, m):
                k = HIDDEN.index((kind, g, m))
                if kind == "z":
                    pool.wait_ge(z_high, b * 2 * KT + (g * KT + m + 1) + CREDIT)
                else:
                    pool.wait_ge(l0_act_done, after(b, L0_ACT, (kind, g, m)))
                high, low = pair[kind, g]
                pool.tensor_tensor(low[:, m, :], plain[:, k % NPLAIN, :], high[:, m, :].bitcast(F32),
                                   ALU.subtract).then_inc(hidden_low, 1)

            def weigh_states(b, gr):
                if gr == 0:
                    pool.wait_ge(l1_act_done, after(b, L1_ACT, ("C", 1)))
                    pool.wait_ge(y_full, b * NGRP + CREDIT)
                if gr == NGRP - 1:
                    pool.wait_ge(states_ready, b * 2 * NGRP + (2 * gr + 1) + CREDIT)
                    pool.wait_ge(y_full, b * NGRP + (gr - 1) + CREDIT)
                    pool.tensor_tensor(pr[:, gr % 2, hs_(0)], hs[:, gr % 2, hs_(0)], Ct[:, hs_(0)], ALU.mult).then_inc(p_half, 1)
                    pool.wait_ge(states_ready, b * 2 * NGRP + (2 * gr + 2) + CREDIT)
                    pool.tensor_tensor(pr[:, gr % 2, hs_(1)], hs[:, gr % 2, hs_(1)], Ct[:, hs_(1)], ALU.mult).then_inc(p_ready, 1)
                    return
                pool.wait_ge(states_ready, b * 2 * NGRP + (2 * gr + 2) + CREDIT)
                if gr >= 2:
                    pool.wait_ge(y_full, b * NGRP + (gr - 1) + CREDIT)
                pool.tensor_tensor(pr[:, gr % 2, :], hs[:, gr % 2, :], Ct[:], ALU.mult).then_inc(p_ready, 1)

            def head(b0, b1):
                if b0 is not None:
                    for g in range(2):
                        scale_q(b0, g)
                    for m in range(KT):
                        low_hidden(b0, "z", 0, m)
                    for m in range(KT):
                        low_hidden(b0, "h1", 0, m)

            def slot(b0, b1, following, k):
                if b0 is not None and k == NGRP - 1:
                    rstd_l1(b0)
                if b1 is not None:
                    weigh_states(b1, k)
                if b0 is not None:
                    for job in HIDDEN_IN_SLOT[k]:
                        low_hidden(b0, *job)
                if following is not None and k == RSTD_L0:
                    rstd_l0(following)

            def stage(b0, b1, following):
                head(b0, b1)
                for k in range(NGRP):
                    slot(b0, b1, following, k)
                if following is not None:
                    for g in range(2):
                        low_xn(following, g)

            pool.wait_ge(consts_set, 4)
            for semaphore in (eps0, rstd0_ready, qg_ready, eps1, rstd1_ready, p_ready, xn_low, hidden_low, p_half):
                pool.sem_inc(semaphore, CREDIT)
            rstd_l0(0)
            for i in (1, 2):
                raw, high, low = FFN_WEIGHTS[i]
                pool.wait_ge(weight_high, i + 1)
                pool.tensor_tensor(low, raw, high.bitcast(F32), ALU.subtract).then_inc(weight_low_h, 1)
            for g in range(2):
                low_xn(0, g)
            stage(0, None, 1)
            with pool.Fori(0, BATCH - 2) as b:
                stage(b + 1, b, b + 2)
            stage(BATCH - 1, BATCH - 2, None)
            stage(None, BATCH - 1, None)

        @block.scalar
        def _(act):
            act.dma_start(mask[:], decay_mask).then_inc(params, 16)
            act.dma_start(grow[:], gamma_row).then_inc(params, 16)
            for dst, src in ((raw_spr, spread), (lw[:], l1_w), (gat[:], gather), (tri[:], before_mask), (w2l[:], w2_l1)):
                act.dma_start(dst, src).then_inc(l1_params, 16)
            for semaphore in (l0_act_done, l1_act_done, xc_ready, sig_ready, g1_ready, z_high, res_ready, x_high):
                act.sem_inc(semaphore, CREDIT)
            act.wait_ge(params, 16 * NPARAM)
            act.activation(theta1[:], col[:, COLS["theta"]], ACT.Exp, scale=0.0).then_inc(theta_ready, 1)
            act.activation(aexp[:], col[:, COLS["A_log"]], ACT.Exp).then_inc(aexp_ready, 1)
            act.wait_ge(aexp_ready, 1)
            act.activation(decay[:], aexp[:], ACT.Exp, scale=-1.0).then_inc(decay_ready, 1)
            def high_weights(i):
                raw, high, _ = FFN_WEIGHTS[i]
                act.wait_ge(raw_loaded[i], 16)
                act.activation(high, raw, ACT.Copy).then_inc(weight_high, 1)

            def full0(b, job):
                act.wait_ge(l0_act_full, after(b, L0_ACT, job))
                return bank0a[L0_ACT.index(job) % 2]

            def take1(b, job, out_ap, func=ACT.Copy, **kw):
                act.wait_ge(l1_act_full, after(b, L1_ACT, job))
                act.activation(out_ap, bank1a[:], func, **kw).then_inc(l1_act_done, 1)

            def plain_free(eng, b, k):
                if k >= NPLAIN:
                    eng.wait_ge(hidden_low, b * len(HIDDEN) + (k - NPLAIN + 1) + CREDIT)
                else:
                    eng.wait_ge(hidden_low, b * len(HIDDEN) + CREDIT)

            def hidden(b, kind, g, m):
                k = HIDDEN.index((kind, g, m))
                plain_free(act, b, k)
                bank = full0(b, (kind, g, m))
                act.activation(plain[:, k % NPLAIN, :], bank[:], ACT.Gelu, scale=scale(kind + "_s", m))
                act.activation(pair[kind, g][0][:, m, :], bank[:], ACT.Gelu,
                               scale=scale(kind + "_s", m)).then_inc(l0_act_done, 1)

            def z_silu(b, g, m):
                k = HIDDEN.index(("z", g, m))
                plain_free(act, b, k)
                bank = full0(b, ("z1", g, m))
                act.activation(plain[:, k % NPLAIN, :], bank[:], ACT.Silu, scale=scale("w1_s", m)).then_inc(l0_act_done, 1)

            def z_round(b, g, m):
                k = HIDDEN.index(("z", g, m))
                act.wait_ge(l0_dve_done, after(b, L0_DVE, ("z2", g, m)))
                act.activation(pair["z", g][0][:, m, :], plain[:, k % NPLAIN, :], ACT.Copy).then_inc(z_high, 1)

            def gate_l0(b, g):
                bank = full0(b, ("w3", g))
                act.activation(g0[:, hs_(g)], bank[:], ACT.Silu, scale=scale("w3_s")).then_inc(l0_act_done, 1)

            def retention_in(b):
                for g in range(2):
                    bank = full0(b, ("xnT", g))
                    act.activation(xnT[:, hs_(g)], bank[:], ACT.Copy)
                    act.activation(xnTh[:, hs_(g)], bank[:], ACT.Copy).then_inc(l0_act_done, 1)

            def retention_q(b, g):
                act.wait_ge(l0_dve_full, b * len(L0_DVE) + CREDIT)
                bank = full0(b, ("q", g))
                act.activation(q[:, hs_(g)], bank[:], ACT.Copy).then_inc(l0_act_done, 1)

            def take_u(b, g):
                bank = full0(b, ("u", g))
                act.activation(u[:, hs_(g)], bank[:], ACT.Copy).then_inc(l0_act_done, 1)

            def head(b0, b1):
                if b0 is not None:
                    z_silu(b0, 0, 0)
                    for m in range(1, KT):
                        z_silu(b0, 0, m)
                        z_round(b0, 0, m - 1)
                        if m >= 2:
                            take_u(b0, m - 2)
                    z_round(b0, 0, KT - 1)
                if b1 is not None:
                    act.wait_ge(conv_step, b1 * TAPS + TAPS + CREDIT)
                    act.activation(xc[:], cv[(TAPS - 1) % 2][:], ACT.Silu, bias=scale("conv_b")).then_inc(xc_ready, 1)
                if b1 is not None:
                    for g in range(2):
                        take1(b1, ("gate", g), gate[:, hs_(g)], ACT.Silu, bias=scale("b_in", 1))
                    act.wait_ge(xc_ready, b1 + 1 + CREDIT)
                    for half in range(2):
                        rows = slice(half * P // 2, (half + 1) * P // 2)
                        last = act.activation(xpair[rows, half, :], xc[rows, :], ACT.Copy)
                    last.then_inc(x_high, 1)
                    act.wait_ge(o_ready, b1 * 2 + CREDIT)
                    act.activation(g1[:], srow[:], ACT.Tanh, scale=0.5).then_inc(sig_ready, 1)
                for k in range(2, CH):
                    if b1 is not None and k >= 4:
                        job, to = (("B", Bt), ("C", Ct))[(k - 4) // 2]
                        take1(b1, (job, k % 2), to[:, hs_(k % 2)], ACT.Identity, bias=scale("b_x", (k - 4) // 2))
                    if b0 is not None and k < 2 + KT:
                        hidden(b0, "h1", 0, k - 2)
                if b1 is not None:
                    act.wait_ge(x1_ready, b1 * 2 + (2 + CREDIT))
                    act.wait_ge(stored, b1 * 32 + CREDIT)
                    act.activation(res[:], x1[:], ACT.Copy).then_inc(res_ready, 1)

            def slot(b0, b1, k):
                if b1 is not None:
                    for g, m in mod_up_in_slot(k, b0 is None):
                        if g == 0:
                            act.wait_ge(l1_dve_full, b1 * len(L1_DVE) + CREDIT)
                        else:
                            act.wait_ge(l1_dve_full, after(b1, L1_DVE, ("ffn", 0)))
                        take1(b1, ("ffn", g, m), fh[:, m, :], ACT.Gelu_apprx_tanh, bias=scale("b1", m))
                if b0 is not None:
                    for kind, g, m in HIDDEN_IN_SLOT[k]:
                        if kind != "z":
                            hidden(b0, kind, g, m)
                            continue
                        z_silu(b0, g, m)
                        if m > 0:
                            z_round(b0, g, m - 1)
                        if m == KT - 1:
                            z_round(b0, g, m)
                    if k == L0_OUT[0]:
                        act.wait_ge(x1_ready, b0 * 2 + CREDIT)
                        gate_l0(b0, 0)
                    elif k == L0_OUT[1]:
                        gate_l0(b0, 1)
                if b1 is not None and k == MOD_DOWN[1]:
                    for g in range(2):
                        act.wait_ge(mod_ready, b1 * 2 + (g + 1) + CREDIT)
                        act.activation(g1[:, hs_(g)], g1[:, hs_(g)], ACT.Silu).then_inc(g1_ready, 1)
                if b0 is not None and k == TO_TOKENS:
                    for g in range(2):
                        bank = full0(b0, ("tok", g))
                        act.activation(early[:, hs_(g)], bank[:], ACT.Copy).then_inc(l0_act_done, 1)

            def tail(b0, following):
                if following is not None:
                    retention_in(following)
                for g in range(2):
                    if following is not None:
                        retention_q(following, g)
                    if b0 is not None:
                        act.wait_ge(mod_ready, b0 * 2 + CREDIT)
                        take1(b0, ("xnT", g), ynT[:, hs_(g)])
                if b0 is not None:
                    for g in range(2):
                        act.wait_ge(p_ready, b0 * NGRP + CREDIT)
                        take1(b0, ("ssm", g), ssm[:, TAPS - 1 + g * HALF:TAPS - 1 + (g + 1) * HALF], ACT.Identity,
                              bias=scale("b_in"))
                    for g in range(2):
                        take1(b0, ("score", g), srow[:, hs_(g)])

            def stage(b0, b1, following):
                head(b0, b1)
                for k in range(NGRP):
                    slot(b0, b1, k)
                tail(b0, following)

            high_weights(0)
            retention_in(0)
            high_weights(1)
            for g in range(2):
                retention_q(0, g)
            high_weights(2)
            high_weights(3)
            act.wait_ge(l1_params, 16 * NPARAM_L1)
            act.activation(spr[:].rearrange("p k n -> p (k n)"), raw_spr, ACT.Copy).then_inc(spr_ready, 1)
            act.wait_ge(inexact_known, 1)
            act.wait_ge(spr_ready, 1)
            stage(0, None, 1)
            with act.Fori(0, BATCH - 2) as b:
                stage(b + 1, b, b + 2)
            stage(BATCH - 1, BATCH - 2, None)
            stage(None, BATCH - 1, None)

        @block.tensor
        def _(pe):
            def open0a(b, job):
                i = L0_ACT.index(job)
                pe.wait_ge(l0_act_done, b * len(L0_ACT) + (max(i - 1, 0) + CREDIT))
                return bank0a[i % 2]

            def open0d(b, job):
                pe.wait_ge(l0_dve_done, b * len(L0_DVE) + (L0_DVE.index(job) + CREDIT))
                return bank0d

            def open1a(b, job):
                pe.wait_ge(l1_act_done, b * len(L1_ACT) + (L1_ACT.index(job) + CREDIT))
                return bank1a

            def open1d(b, job):
                i = L1_DVE.index(job)
                pe.wait_ge(l1_dve_done, b * len(L1_DVE) + (max(i - 1, 0) + CREDIT))
                return bank1d[i % 2]

            def retention_in(b):
                for g in range(2):
                    pe.wait_ge(xn_ready, b * 2 + (g + 1) + CREDIT)
                    bank = open0a(b, ("xnT", g))
                    for c in range(CPH):
                        last = pe.transpose(bank[:, ck(c)], xn[:, g * CPH + c, :], ident[:])
                    last.then_inc(l0_act_full, 1)

            def retention_q(b, g):
                bank = open0a(b, ("q", g))
                pe.wait_ge(l0_act_done, after(b, L0_ACT, ("xnT", g)))
                pe.matmul(bank[:], qk[:], xnT[:, hs_(g)], start=True, stop=True).then_inc(l0_act_full, 1)

            def scores(b, g):
                bank = open0d(b, ("scores", g))
                pe.wait_ge(l0_act_done, after(b, L0_ACT, ("q", g)))
                for c in range(g * CPH, (g + 1) * CPH):
                    last = pe.matmul(bank[:, ck(c - g * CPH)], xnT[:, ck(c)], q[:, ck(c)], start=True, stop=True)
                last.then_inc(l0_dve_full, 1)

            def outer(b, g):
                pe.wait_ge(xg_ready, b + 1 + CREDIT)
                bank = open0d(b, ("outer", g))
                for c in range(g * CPH, (g + 1) * CPH):
                    last = pe.matmul(bank[:, ck(c - g * CPH)], xg[:, c, :], xn[:, c, :], start=True, stop=True)
                last.then_inc(l0_dve_full, 1)

            def retention_out(b, g):
                bank = open0a(b, ("u", g))
                pe.wait_ge(qg_ready, b * 2 + (g + 1) + CREDIT)
                pe.wait_ge(l0_dve_done, after(b, L0_DVE, ("outer", g)))
                for c in range(g * CPH, (g + 1) * CPH):
                    pe.matmul(bank[:, ck(c - g * CPH)], xn[:, c, :], sc[:, c, :], start=True, stop=False)
                    last = pe.matmul(bank[:, ck(c - g * CPH)], mem[:, c, :], qg[:, ck(c)], start=False, stop=True)
                last.then_inc(l0_act_full, 1)

            def value(b, g):
                bank = open0d(b, ("s", g))
                pe.wait_ge(l0_act_done, after(b, L0_ACT, ("u", g)))
                pe.matmul(bank[:], rw[:, 2, :], u[:, hs_(g)], start=True, stop=True).then_inc(l0_dve_full, 1)

            def rest(exact):
                def split_product(bank, terms, start=True, stop=True):
                    passes = []
                    for wh, wl, xh, xl in terms:
                        passes += [(wh, xh), (wh, xl)] if exact else [(wh, xh), (wh, xl), (wl, xh)]
                    for n, (w, x) in enumerate(passes):
                        last = pe.matmul(bank[:], w, x, start=(start and n == 0), stop=(stop and n == len(passes) - 1))
                    return last

                def z1(b, g, m):
                    pe.wait_ge(xn_low, b * 2 + (g + 1) + CREDIT)
                    bank = open0a(b, ("z1", g, m))
                    split_product(bank, [(w12h[:, 0, ck(m)], w12l[:, 0, ck(m)], xnTh[:, hs_(g)],
                                          xnTl[:, hs_(g)])]).then_inc(l0_act_full, 1)

                def z2(b, g, m):
                    pe.wait_ge(xn_low, b * 2 + (g + 1) + CREDIT)
                    bank = open0d(b, ("z2", g, m))
                    split_product(bank, [(w12h[:, 1, ck(m)], w12l[:, 1, ck(m)], xnTh[:, hs_(g)],
                                          xnTl[:, hs_(g)])]).then_inc(l0_dve_full, 1)

                def split_ready(b, kind, g, m):
                    pe.wait_ge(hidden_low, b * len(HIDDEN) + (HIDDEN.index((kind, g, m)) + 1 + CREDIT))

                def hidden_terms(kind, g, m, kts):
                    i = ("h1", "h2").index(kind)
                    high, low = pair[("z", "h1")[i], g]
                    return [(hTh[:, i, kt, ck(m)], hTl[:, i, kt, ck(m)], high[:, kt, :], low[:, kt, :]) for kt in kts]

                def hidden(b, kind, g, m):
                    bank = open0a(b, (kind, g, m))
                    split_ready(b, {"h1": "z", "h2": "h1"}[kind], g, KT - 1)
                    split_product(bank, hidden_terms(kind, g, m, range(KT))).then_inc(l0_act_full, 1)

                def first_hidden(b, kind, g):
                    for kts in ((0, 1), (2,), (3,)):
                        split_ready(b, {"h1": "z", "h2": "h1"}[kind], g, kts[-1])
                        for m in range(2):
                            if kts[0] == 0:
                                open0a(b, (kind, g, m))
                            last = split_product(bank0a[L0_ACT.index((kind, g, m)) % 2], hidden_terms(kind, g, m, kts),
                                                 kts[0] == 0, kts[-1] == KT - 1)
                            if kts[-1] == KT - 1:
                                last.then_inc(l0_act_full, 1)

                def ffn_out(b, g):
                    bank = open0a(b, ("w3", g))
                    high, low = pair["h2", g]
                    for kt in range(KT):
                        split_ready(b, "h2", g, kt)
                        last = split_product(bank, [(w3h[:, kt, :], w3l[:, kt, :], high[:, kt, :], low[:, kt, :])],
                                             kt == 0, kt == KT - 1)
                    last.then_inc(l0_act_full, 1)

                def project(b, job, g, w, source=ynT):
                    bank = open1a(b, (job, g))
                    pe.matmul(bank[:], w, source[:, hs_(g)], start=True, stop=True).then_inc(l1_act_full, 1)

                def to_tokens(b):
                    for g in range(2):
                        bank = open0a(b, ("tok", g))
                        pe.wait_ge(x1_ready, b * 2 + (g + 1) + CREDIT)
                        for c in range(CPH):
                            last = pe.transpose(bank[:, ck(c)], x1[:, ck(g * CPH + c)], ident[:])
                        last.then_inc(l0_act_full, 1)

                def norm_to_features(b, g):
                    bank = open1a(b, ("xnT", g))
                    pe.wait_ge(yn_ready, b * 2 + (g + 1) + CREDIT)
                    for c in range(CPH):
                        last = pe.transpose(bank[:, ck(c)], yn[:, g * CPH + c, :], ident[:])
                    last.then_inc(l1_act_full, 1)

                def score_column(b, g):
                    bank = open1d(b, ("score_col", g))
                    pe.wait_ge(l1_act_done, after(b, L1_ACT, ("score", g)))
                    for c in range(CPH):
                        last = pe.transpose(bank[:, ck(c)], srow[:, ck(g * CPH + c)], ident[:])
                    last.then_inc(l1_dve_full, 1)

                def rank(b, c, banks):
                    pe.wait_ge(beats_ready, b * CH + (c + 1) + CREDIT)
                    for g in range(2):
                        last = pe.matmul(banks[g][:], ones[:], beats[:, c % 2, hs_(g)],
                                         start=(c == 0), stop=(c == CH - 1))
                        if c == CH - 1:
                            last.then_inc(l1_dve_full, 1)
                    if c < CH - 1:
                        last.then_inc(ranked, 1)

                def mod_up(b, g, m):
                    bank = open1a(b, ("ffn", g, m))
                    pe.matmul(bank[:], W_1[:, ck(m)], ynT[:, hs_(g)], start=True, stop=True).then_inc(l1_act_full, 1)

                def mod_down(b, g):
                    bank = open1d(b, ("ffn", g))
                    pe.wait_ge(l1_act_done, after(b, L1_ACT, ("ffn", g, KT - 1)))
                    for kt in range(KT):
                        last = pe.matmul(bank[:], w2l[:, kt, :], fh[:, kt, :], start=(kt == 0), stop=(kt == KT - 1))
                    last.then_inc(l1_dve_full, 1)

                def spread_x(b, gr):
                    half, k = divmod(gr, NGRP // 2)
                    if gr == 0:
                        pe.wait_ge(x_low, b + 1 + CREDIT)
                    for g in range(2):
                        bank = open1d(b, ("xs", gr, g))
                        pe.matmul(bank[:], spr[:, k, :], xpair[:, half, hs_(g)], start=True, stop=True).then_inc(l1_dve_full, 1)

                def gather_y(b, gr, g):
                    if gr == 0:
                        pe.wait_ge(yd_ready, b * 2 + CREDIT)
                    if gr == NGRP - 1 and g == 0:
                        pe.wait_ge(p_half, b + 1 + CREDIT)
                    else:
                        pe.wait_ge(p_ready, b * NGRP + (gr + 1) + CREDIT)
                    last = pe.matmul(ybank[g][:], gat[:, P - DPG * (gr + 1):2 * P - DPG * (gr + 1)],
                                     pr[:, gr % 2, hs_(g)], start=(gr == 0), stop=(gr == NGRP - 1))
                    if g == 1:
                        last.then_inc(y_full, 1)
                    elif gr == NGRP - 1:
                        last.then_inc(y_half, 1)

                def fill(b0, b1, k):
                    if b1 is not None and k < 2:
                        project(b1, "gate", k, W_IN[:, P:2 * P])
                    if b1 is not None and k >= 4:
                        if k == 4:
                            pe.wait_ge(xc_ready, b1 + 1 + CREDIT)
                        job, w = (("B", W_B), ("C", W_C))[(k - 4) // 2]
                        project(b1, job, k % 2, w, xc)
                    if b1 is None and k == 2:
                        first_hidden(b0, "h1", 0)
                    elif b0 is not None and 2 + (2 if b1 is None else 0) <= k < 2 + KT:
                        hidden(b0, "h1", 0, k - 2)

                def head(b0, b1, first=False):
                    for g in range(2):
                        if b0 is not None and (first or g == 1):
                            z1(b0, 0, g)
                        if b1 is not None:
                            score_column(b1, g)
                        if b0 is not None and not first and g == 0:
                            outer(b0, 0)
                    if b0 is not None:
                        if not first:
                            scores(b0, 1)
                        z1(b0, 0, 2)
                        if not first:
                            outer(b0, 1)
                        z2(b0, 0, 0)
                        retention_out(b0, 0)
                        z2(b0, 0, 1)
                        z1(b0, 0, 3)
                        z2(b0, 0, 2)
                        retention_out(b0, 1)
                        z2(b0, 0, 3)
                    if b1 is not None:
                        banks = [open1d(b1, ("rank", g)) for g in range(2)]
                    for c in range(CH):
                        fill(b0, b1, c)
                        if b1 is not None:
                            rank(b1, c, banks)
                    if b1 is not None and b0 is None:
                        spread_x(b1, 0)

                def slot(b0, b1, following, k):
                    def next_inputs():
                        if b1 is not None and k < NGRP - 1:
                            spread_x(b1, k + 1)

                    def sum_states(g):
                        if b1 is not None and k > 0:
                            gather_y(b1, k - 1, g)

                    if b1 is not None and k in MOD_DOWN:
                        mod_down(b1, MOD_DOWN.index(k))
                    if b0 is None:
                        next_inputs()
                        for g in range(2):
                            sum_states(g)
                        for g, m in mod_up_in_slot(k, True):
                            mod_up(b1, g, m)
                        return
                    jobs = HIDDEN_IN_SLOT[k]
                    if jobs and jobs[0][0] == "z":
                        (_, g, m), _ = jobs
                        z1(b0, g, m)
                        z2(b0, g, m)
                        z1(b0, g, m + 1)
                        next_inputs()
                        sum_states(0)
                        z2(b0, g, m + 1)
                        sum_states(1)
                        return
                    if b1 is not None and k in MOD_UP:
                        g = MOD_UP.index(k)
                        mod_up(b1, g, 0)
                        mod_up(b1, g, 1)
                        sum_states(0)
                        mod_up(b1, g, 2)
                        sum_states(1)
                        mod_up(b1, g, 3)
                        next_inputs()
                        return
                    if jobs and b1 is None and jobs[0][2] == 0:
                        first_hidden(b0, *jobs[0][:2])
                    elif jobs:
                        hidden(b0, *jobs[0])
                        if k == 0 and b1 is not None:
                            spread_x(b1, 0)
                        hidden(b0, *jobs[1])
                    if k in L0_OUT:
                        ffn_out(b0, L0_OUT.index(k))
                        value(b0, L0_OUT.index(k))
                    elif k == TO_TOKENS:
                        to_tokens(b0)
                    elif k == NGRP - 1 and following is not None:
                        retention_in(following)
                    next_inputs()
                    for g in range(2):
                        sum_states(g)

                def project_out(b, g):
                    bank = open1d(b, ("out", g))
                    pe.wait_ge(yg_ready, b * 2 + (g + 1) + CREDIT)
                    pe.matmul(bank[:], W_OUT, yg[:, hs_(g)], start=True, stop=True).then_inc(l1_dve_full, 1)

                def tail(b0, b1, following):
                    for g in range(2):
                        if following is not None:
                            retention_q(following, g)
                        if b0 is not None:
                            norm_to_features(b0, g)
                    if b1 is not None:
                        for g in range(2):
                            gather_y(b1, NGRP - 1, g)
                    for g in range(2):
                        if b0 is not None:
                            pe.wait_ge(l1_act_done, after(b0, L1_ACT, ("xnT", g)))
                            project(b0, "ssm", g, W_IN[:, 0:P])
                        if following is not None and g == 0:
                            scores(following, 0)
                        if b1 is not None:
                            project_out(b1, g)
                    if b0 is not None:
                        for g in range(2):
                            project(b0, "score", g, W_R)
                            if following is not None and g == 0:
                                z1(following, 0, 0)

                def stage(b0, b1, following, first=False):
                    head(b0, b1, first)
                    for k in range(NGRP):
                        slot(b0, b1, following, k)
                    tail(b0, b1, following)

                stage(0, None, 1, first=True)
                with pe.Fori(0, BATCH - 2) as b:
                    stage(b + 1, b, b + 2)
                stage(BATCH - 1, BATCH - 2, None)
                stage(None, BATCH - 1, None)

            for semaphore in (l0_act_full, l0_dve_full, l1_act_full, l1_dve_full, y_full, y_half, ranked):
                pe.sem_inc(semaphore, CREDIT)
            pe.wait_ge(wk_ready, 1)
            pe.matmul(bank0d[:, 0:P], rw[:, 0, :], wk_th[:], start=True, stop=True).then_inc(qk_full, 1)
            pe.wait_ge(qk_ready, 1)
            retention_in(0)
            for g in range(2):
                retention_q(0, g)
            for g in range(2):
                scores(0, g)
                outer(0, g)
            pe.wait_ge(consts_set, 4)
            pe.wait_ge(l1_params, 16 * NPARAM_L1)
            pe.wait_ge(inexact_ready, 1)
            pe.matmul(bank1a[:, 0:len(FFN_WEIGHTS)], ones[:], inexact_b[:], start=True, stop=True).then_inc(inexact_full, 1)
            pe.wait_ge(inexact_known, 1)
            has_low = pe.value_load(inexact_i[0:1, 0:1], min_val=0, max_val=P * len(FFN_WEIGHTS))
            with pe.If(has_low):
                rest(exact=False)
            with pe.Else():
                rest(exact=True)

        @block.vector
        def _(dve):
            for semaphore in (stats0, aggr0, xn_ready, xg_ready, l0_dve_done, mem_step, x1_ready, stats1, aggr1,
                              l1_dve_done, tie_ready, beats_ready, sigh_ready, conv_step, mod_ready,
                              yd_ready, yg_ready, o_ready, x_low, pad_ready,
                              yn_ready, states_ready):
                dve.sem_inc(semaphore, CREDIT)

            def full0(b, job):
                dve.wait_ge(l0_dve_full, after(b, L0_DVE, job))

            def full1(b, job):
                dve.wait_ge(l1_dve_full, after(b, L1_DVE, job))
                return bank1d[L1_DVE.index(job) % 2]

            def stats_l0(b):
                dve.wait_ge(x_tok_in, b * 16 + 16)
                for c in range(CH):
                    last = dve.bn_stats(st0[:, c, :], xt[:, c, :])
                last.then_inc(stats0, 1)
                dve.wait_ge(stats0, b + 1 + CREDIT)
                dve.memset(wait_carrier[:, 2:3], 0.0)
                for c in range(CH):
                    last = dve.bn_aggr(mv0[:, c, :], st0[:, c, :])
                last.then_inc(aggr0, 1)

            def norm_l0(b):
                dve.wait_ge(aggr0, b + 1 + CREDIT)
                dve.wait_ge(rstd0_ready, b + 1 + CREDIT)
                for g in range(2):
                    for c in range(g * CPH, (g + 1) * CPH):
                        last = dve.tensor_scalar(xn[:, c, :], xt[:, c, :], mv0[:, c, 0:1], rstd0[:, c:c + 1],
                                                 ALU.subtract, ALU.mult)
                    last.then_inc(xn_ready, 1)
                dve.wait_ge(xn_ready, b * 2 + 2 + CREDIT)
                if isinstance(b, int) and b == 0:
                    dve.wait_ge(params, 16 * NPARAM)
                dve.tensor_scalar(xg[:], xn[:], scale("gamma_col"), None, ALU.mult).then_inc(xg_ready, 1)

            def mask_scores(b, g):
                cs = slice(g * CPH, (g + 1) * CPH)
                full0(b, ("scores", g))
                dve.tensor_tensor(sc[:, cs, :], bank0d[:].rearrange("p (c i) -> p c i", i=P),
                                  mask[:].rearrange("p (o i) -> p o i", o=1).broadcast_to([P, CPH, P]),
                                  ALU.mult).then_inc(l0_dve_done, 1)

            def memory(b, g):
                full0(b, ("outer", g))
                for c in range(g * CPH, (g + 1) * CPH):
                    if c == CPH:
                        dve.wait_ge(l0_dve_done, after(b, L0_DVE, ("outer", 0)))
                    elif c > 0:
                        dve.wait_ge(mem_step, b * MEM_STEPS + (c - g) + CREDIT)
                    last = dve.scalar_tensor_tensor(mem[:, c + 1, :], mem[:, c, :], GAMMA ** P,
                                                    bank0d[:, ck(c - g * CPH)], ALU.mult, ALU.add)
                    if c + 1 in ((g + 1) * CPH, CH - 1):
                        last.then_inc(l0_dve_done, 1)
                        break
                    last.then_inc(mem_step, 1)

            def z_product(b, g, m):
                k = HIDDEN.index(("z", g, m))
                full0(b, ("z2", g, m))
                dve.wait_ge(l0_act_done, after(b, L0_ACT, ("z1", g, m)))
                dve.scalar_tensor_tensor(plain[:, k % NPLAIN, :], bank0d[:], scale("w2_s", m), plain[:, k % NPLAIN, :],
                                         ALU.mult, ALU.mult).then_inc(l0_dve_done, 1)

            def residual_l0(b, g):
                full0(b, ("s", g))
                dve.wait_ge(l0_act_done, after(b, L0_ACT, ("w3", g)))
                dve.wait_ge(res_ready, b + CREDIT)
                dve.tensor_tensor(sg[:, hs_(g)], bank0d[:], g0[:, hs_(g)], ALU.mult).then_inc(l0_dve_done, 1)
                dve.wait_ge(l0_dve_done, after(b, L0_DVE, ("s", g)))
                dve.wait_ge(x_feat_in, b * 16 + 16)
                dve.tensor_tensor(x1[:, hs_(g)], sg[:, hs_(g)], xf[:, hs_(g)], ALU.add).then_inc(x1_ready, 1)

            def stats_l1(b):
                for g in range(2):
                    dve.wait_ge(l0_act_done, after(b, L0_ACT, ("tok", g)))
                    for c in range(g * CPH, (g + 1) * CPH):
                        last = dve.bn_stats(st1[:, c, :], yn[:, c, :])
                    last.then_inc(stats1, 1)
                for g in range(2):
                    dve.wait_ge(stats1, b * 2 + (g + 1) + CREDIT)
                    dve.memset(wait_carrier[:, g:g + 1], 0.0)
                    for c in range(g * CPH, (g + 1) * CPH):
                        last = dve.bn_aggr(mv1[:, c, :], st1[:, c, :])
                    last.then_inc(aggr1, 1)

            def norm_l1(b):
                for g in range(2):
                    dve.wait_ge(rstd1_ready, b * 2 + (g + 1) + CREDIT)
                    dve.wait_ge(aggr1, b * 2 + (g + 1) + CREDIT)
                    for c in range(g * CPH, (g + 1) * CPH):
                        last = dve.tensor_scalar(yn[:, c, :], yn[:, c, :], mv1[:, c, 0:1], rstd1[:, c:c + 1],
                                                 ALU.subtract, ALU.mult)
                    last.then_inc(yn_ready, 1)

            def pad(b):
                dve.wait_ge(p_ready, b * NGRP + CREDIT)
                dve.memset(ssm[:, 0:TAPS - 1], 0.0).then_inc(pad_ready, 1)

            def score_columns(b):
                for g in range(2):
                    bank = full1(b, ("score_col", g))
                    dve.tensor_copy(scol[:, g * CPH:(g + 1) * CPH],
                                    bank[:].rearrange("p (c i) -> p c i", i=P)[:, :, 0]).then_inc(l1_dve_done, 1)

            def convolve(b, k):
                if k == 0:
                    dve.wait_ge(l1_act_done, after(b, L1_ACT, ("ssm", 1)))
                    dve.wait_ge(pad_ready, b + 1 + CREDIT)
                    dve.tensor_scalar(cv[0][:], ssm[:, 0:SEQ], scale("conv_w", 0), None, ALU.mult).then_inc(conv_step, 1)
                else:
                    dve.wait_ge(conv_step, b * TAPS + k + CREDIT)
                    dve.scalar_tensor_tensor(cv[k % 2][:], ssm[:, k:k + SEQ], scale("conv_w", k), cv[(k + 1) % 2][:],
                                             ALU.mult, ALU.add).then_inc(conv_step, 1)

            def low_x(b):
                dve.wait_ge(x_high, b + 1 + CREDIT)
                for half in range(2):
                    rows = slice(half * P // 2, (half + 1) * P // 2)
                    other = slice((1 - half) * P // 2, (2 - half) * P // 2)
                    last = dve.tensor_tensor(xpair[other, half, :], xc[rows, :], xpair[rows, half, :].bitcast(F32),
                                             ALU.subtract)
                last.then_inc(x_low, 1)

            def ties(b):
                dve.wait_ge(l1_dve_done, after(b, L1_DVE, ("score_col", 1)))
                for c in range(CH):
                    dve.scalar_tensor_tensor(tie[:, c, :], srow[:, ck(c)], scol[:, c:c + 1], tri[:],
                                             ALU.is_equal, ALU.mult).then_inc(tie_ready, 1)

            def compare(b):
                for c in range(CH):
                    if c == CH // 2:
                        dve.wait_ge(sig_ready, b + 1 + CREDIT)
                        dve.tensor_scalar(g1[:], g1[:], 0.5, 0.5, ALU.mult, ALU.add).then_inc(sigh_ready, 1)
                    if c >= 2:
                        dve.wait_ge(ranked, b * (CH - 1) + (c - 1) + CREDIT)
                    s_i = scol[:, c:c + 1]
                    bt = beats[:, c % 2, :]
                    if c > 0:
                        dve.tensor_scalar(bt[:, 0:c * P], srow[:, 0:c * P], s_i, None, ALU.is_lt)
                    if c < CH - 1:
                        dve.tensor_scalar(bt[:, (c + 1) * P:], srow[:, (c + 1) * P:], s_i, None, ALU.is_le)
                    dve.wait_ge(tie_ready, b * CH + (c + 1) + CREDIT)
                    dve.scalar_tensor_tensor(bt[:, ck(c)], srow[:, ck(c)], s_i, tie[:, c, :],
                                             ALU.is_lt, ALU.add).then_inc(beats_ready, 1)

            def token_weights(b):
                dve.wait_ge(sigh_ready, b + 1 + CREDIT)
                for g in range(2):
                    bank = full1(b, ("rank", g))
                    dve.scalar_tensor_tensor(g1[:, hs_(g)], bank[:], float(TOPK), g1[:, hs_(g)],
                                             ALU.is_lt, ALU.mult).then_inc(l1_dve_done, 1)

            def mod_update(b, g):
                bank = full1(b, ("ffn", g))
                dve.wait_ge(l1_dve_done, after(b, L1_DVE, ("rank", g)))
                dve.scalar_tensor_tensor(g1[:, hs_(g)], bank[:], scale("b2"), g1[:, hs_(g)],
                                         ALU.add, ALU.mult).then_inc(l1_dve_done, 1)
                dve.wait_ge(l1_dve_done, after(b, L1_DVE, ("ffn", g)))
                dve.tensor_tensor(g1[:, hs_(g)], g1[:, hs_(g)], ynT[:, hs_(g)], ALU.add).then_inc(mod_ready, 1)

            def states(b, gr):
                if gr == 0:
                    dve.wait_ge(l1_act_done, after(b, L1_ACT, ("B", 1)))
                h = hs[:, gr % 2, :]
                dve.wait_ge(p_ready, b * NGRP + (max(gr - 1, 0) + CREDIT))
                for g in range(2):
                    bank = full1(b, ("xs", gr, g))
                    dve.tensor_tensor(h[:, hs_(g)], bank[:], Bt[:, hs_(g)], ALU.mult).then_inc(l1_dve_done, 1)
                for g in range(2):
                    dve.wait_ge(l1_dve_done, after(b, L1_DVE, ("xs", gr, g)))
                    if g == 1:
                        dve.wait_ge(states_ready, b * 2 * NGRP + (2 * gr + 1) + CREDIT)
                    dve.tensor_tensor_scan(h[:, hs_(g)], decay[:, gr:gr + 1].broadcast_to([P, HALF]), h[:, hs_(g)],
                                           0.0 if g == 0 else h[:, HALF - 1:HALF],
                                           ALU.mult, ALU.add).then_inc(states_ready, 1)

            def gate_y(b):
                for g in range(2):
                    if g == 0:
                        dve.wait_ge(y_half, b + 1 + CREDIT)
                    else:
                        dve.wait_ge(y_full, b * NGRP + NGRP + CREDIT)
                    dve.scalar_tensor_tensor(yg[:, hs_(g)], xc[:, hs_(g)], scale("D"), ybank[g][:],
                                             ALU.mult, ALU.add).then_inc(yd_ready, 1)
                for g in range(2):
                    dve.wait_ge(yd_ready, b * 2 + (g + 1) + CREDIT)
                    dve.tensor_tensor(yg[:, hs_(g)], yg[:, hs_(g)], gate[:, hs_(g)], ALU.mult).then_inc(yg_ready, 1)

            def output(b):
                for g in range(2):
                    bank = full1(b, ("out", g))
                    dve.wait_ge(g1_ready, b * 2 + (g + 1) + CREDIT)
                    dve.scalar_tensor_tensor(g1[:, hs_(g)], bank[:], scale("b_out"), g1[:, hs_(g)],
                                             ALU.add, ALU.mult).then_inc(l1_dve_done, 1)
                for g in range(2):
                    dve.wait_ge(l1_dve_done, after(b, L1_DVE, ("out", g)))
                    dve.wait_ge(res_ready, b + 1 + CREDIT)
                    dve.tensor_tensor(res[:, hs_(g)], g1[:, hs_(g)], res[:, hs_(g)], ALU.add).then_inc(o_ready, 1)

            def head(b0, b1, first=False):
                for g in range(2):
                    if b0 is not None and not first:
                        mask_scores(b0, g)
                    if b1 is not None:
                        convolve(b1, 2 * g)
                    if b0 is not None and not first:
                        memory(b0, g)
                    if b1 is not None:
                        convolve(b1, 2 * g + 1)
                if b0 is not None:
                    z_product(b0, 0, 0)
                if b1 is not None:
                    score_columns(b1)
                if b0 is not None:
                    z_product(b0, 0, 1)
                if b1 is not None:
                    ties(b1)
                if b0 is not None:
                    z_product(b0, 0, 2)
                    z_product(b0, 0, 3)
                if b1 is not None:
                    compare(b1)
                    low_x(b1)
                    token_weights(b1)

            def slot(b0, b1, following, k):
                if b1 is not None:
                    states(b1, k)
                    if k in MOD_DOWN:
                        mod_update(b1, MOD_DOWN.index(k))
                if b0 is not None:
                    for kind, g, m in HIDDEN_IN_SLOT[k]:
                        if kind == "z":
                            z_product(b0, g, m)
                    if k in L0_OUT:
                        residual_l0(b0, L0_OUT.index(k))
                    elif k == TO_TOKENS:
                        stats_l1(b0)
                    elif k == NGRP - 1:
                        norm_l1(b0)
                if following is not None:
                    if k == STATS_L0:
                        stats_l0(following)
                    elif k == NORM_L0:
                        norm_l0(following)

            def stage(b0, b1, following, first=False):
                head(b0, b1, first)
                for k in range(NGRP):
                    slot(b0, b1, following, k)
                if b1 is not None:
                    gate_y(b1)
                if b0 is not None:
                    pad(b0)
                if b1 is not None:
                    output(b1)

            dve.wait_ge(consts_set, 4)
            stats_l0(0)
            dve.wait_ge(params, 16 * NPARAM)
            dve.wait_ge(theta_ready, 1)
            dve.tensor_scalar(wk_th[:], rw[:, 1, :], theta1[:, 0:1], theta1[:, 0:1], ALU.mult, ALU.mult).then_inc(wk_ready, 1)
            norm_l0(0)
            dve.wait_ge(qk_full, 1)
            dve.tensor_copy(qk[:], bank0d[:, 0:P]).then_inc(qk_ready, 1)
            def low_weights(i):
                raw, high, low = FFN_WEIGHTS[i]
                if i in (1, 2):
                    dve.wait_ge(weight_low_h, i)
                else:
                    dve.wait_ge(weight_high, i + 1)
                    dve.tensor_tensor(low, raw, high.bitcast(F32), ALU.subtract).then_inc(weight_low, 1)
                    dve.wait_ge(weight_low, 1 if i == 0 else 2)
                dve.tensor_reduce(inexact[:, i:i + 1], low.bitcast(F32), mybir.AxisListType.X, ALU.max,
                                  apply_absolute_value=True).then_inc(inexact_step, 1)

            low_weights(0)
            for g in range(2):
                mask_scores(0, g)
                memory(0, g)
            for i in (3, 1, 2):
                low_weights(i)
            dve.wait_ge(inexact_step, len(FFN_WEIGHTS))
            dve.tensor_scalar(inexact_b[:], inexact[:], 0.0, None, ALU.not_equal).then_inc(inexact_ready, 1)
            dve.wait_ge(inexact_full, 1)
            dve.tensor_reduce(inexact[:, 0:1], bank1a[:, 0:len(FFN_WEIGHTS)], mybir.AxisListType.X, ALU.add).then_inc(inexact_step, 1)
            dve.wait_ge(inexact_step, len(FFN_WEIGHTS) + 1)
            dve.tensor_copy(inexact_i[:], inexact[:, 0:1]).then_inc(inexact_known, 1)
            dve.wait_ge(l1_params, 16 * NPARAM_L1)
            dve.wait_ge(decay_ready, 1)
            stage(0, None, 1, first=True)
            with dve.Fori(0, BATCH - 2) as b:
                stage(b + 1, b, b + 2)
            stage(BATCH - 1, BATCH - 2, None)
            stage(None, BATCH - 1, None)


def constants():
    i = np.arange(P)
    diff = i[None, :] - i[:, None]
    decay_mask = np.where(diff >= 0, GAMMA ** np.maximum(diff, 0), 0.0)
    gamma_row = np.broadcast_to(GAMMA ** (i + 1.0), (P, P))
    before_mask = (i[:, None] < i[None, :]).astype(np.float32)
    n, dd = i // DPG, i % DPG
    spread = np.zeros((P, NGRP // 2, P), np.float32)
    for g in range(NGRP // 2):
        for part in range(2):
            spread[part * P // 2 + DPG * g + dd, g, i] = 1.0
    gather = np.zeros((P, 2 * P - DPG), np.float32)
    gather[i, P - DPG + dd] = 1.0
    return {"decay_mask": decay_mask.astype(np.float32), "gamma_row": gamma_row.astype(np.float32),
            "identity": np.eye(P, dtype=np.float32), "before_mask": before_mask,
            "spread": spread.reshape(P, -1), "gather": gather,
            "gamma_col": (GAMMA ** (P - 1.0 - i)).astype(np.float32)[:, None]}


def kernel(**inputs):
    import concourse.bacc as bacc
    from concourse.bass_utils import run_bass_kernel_spmd

    a = {k: np.asarray(v) for k, v in inputs.items()}
    c = constants()
    x = a["L0_attn_x"]

    def columns(v):
        return v.reshape(-1, P).T

    def k_tiles(w):
        return w.reshape(-1, P, w.shape[1]).transpose(1, 0, 2)

    a_log = a["L1_attn_A_log"].reshape(NGRP, DPG, NSTATE).transpose(2, 1, 0).reshape(P, NGRP)
    w_x, b_x = a["L1_attn_W_x"], a["L1_attn_b_x"]
    cols = {"w1_s": columns(a["L0_ffn_w1_s"]), "w2_s": columns(a["L0_ffn_w2_s"]), "h1_s": columns(a["L0_ffn_h1_s"]),
            "h2_s": columns(a["L0_ffn_h2_s"]), "w3_s": columns(a["L0_ffn_w3_s"]), "theta": columns(a["L0_attn_theta"]),
            "b_in": columns(a["L1_attn_b_in"]), "conv_w": a["L1_attn_conv_w"], "conv_b": columns(a["L1_attn_conv_b"]),
            "D": columns(a["L1_attn_D_param"]), "b_out": columns(a["L1_attn_b_out"]), "b1": columns(a["L1_ffn_b1"]),
            "b2": columns(a["L1_ffn_b2"]), "b_x": np.repeat(b_x, DPG).reshape(2, P).T, "A_log": a_log,
            "gamma_col": c.pop("gamma_col")}
    arrays = {
        "x_tok": x.reshape(BATCH, CH, P, P).transpose(0, 2, 1, 3),
        "x_feat": x.transpose(0, 2, 1),
        "small": np.concatenate([cols[k] for k in COLS], axis=1),
        "w_in0": np.concatenate([a["L0_ffn_w1_w"].T, a["L0_ffn_w2_w"].T], axis=1),
        "h_w": np.stack([k_tiles(a["L0_ffn_h1_w"].T), k_tiles(a["L0_ffn_h2_w"].T)], axis=1).reshape(P, 2, -1),
        "w3T": k_tiles(a["L0_ffn_w3_w"].T).reshape(P, -1),
        "retention_w": np.stack([a["L0_attn_weight_q"].T, a["L0_attn_weight_k"].T, a["L0_attn_weight_v"]], axis=1),
        "l1_w": np.concatenate([a["L1_attn_W_in"], np.repeat(w_x, DPG, axis=1),
                                np.repeat(a["L1_ffn_w_router"][:, None], P, axis=1), a["L1_attn_W_out"],
                                a["L1_ffn_W1"]], axis=1),
        "w2_l1": k_tiles(a["L1_ffn_W2"]),
        **c,
    }
    nc = bacc.Bacc("TRN2", target_bir_lowering=False, num_devices=1)
    aps = {}
    for name, value in arrays.items():
        arrays[name] = np.ascontiguousarray(value)
        aps[name] = nc.dram_tensor(name, arrays[name].shape, mybir.dt.from_np(arrays[name].dtype),
                                   kind="ExternalInput").ap()
    out = nc.dram_tensor("out", (BATCH, P, SEQ), F32, kind="ExternalOutput").ap()
    program(nc, out=out, **aps)
    got = run_bass_kernel_spmd(nc, [arrays], core_ids=[0]).results[0]["out"]
    return np.ascontiguousarray(got.transpose(0, 2, 1))
```
